# Optimizing a Trainium2 kernel written in Bass

```python
import numpy as np
import jax
import jax.numpy as jnp

def _softmax(x, axis=-1):
    return jax.nn.softmax(x, axis=axis)

def _gelu(x):
    return jax.nn.gelu(x, approximate=True)

def _silu(x):
    return jax.nn.silu(x)

def _sigmoid(x):
    return jax.nn.sigmoid(x)

def _layernorm(x, axis=-1, eps=1e-05):
    m = jnp.mean(x, axis=axis, keepdims=True)
    v = jnp.var(x, axis=axis, keepdims=True)
    return (x - m) / jnp.sqrt(v + eps)

def _scatter_add(tgt, idx, src, axis=0):
    return tgt.at[idx].add(src)

def _segment_sum(src, seg, n):
    return jax.ops.segment_sum(src, seg, n)
kernel_name = 'mk_lm_tower_d1_tok_ids512_r4_d8a1a0'

def setup_inputs(seed: int=0):
    np.random.seed(seed)
    _w = jnp.asarray

    def _rec_inputs():
        import jax
        import jax.numpy as jnp
        _rk = jax.random.key(seed)
        x = jax.random.randint(jax.random.fold_in(_rk, 1), (2, 1024), 0, 12564, jnp.int32)
        return x
    x = _rec_inputs()

    def _L0_tok_setup():
        import jax, jax.numpy as jnp
        import numpy as np
        VOCAB, D, B, S, E = (50257, 128, 8, 512, 5)
        L_CONST = 1000000000.0
        key = jax.random.key(seed)
        k = jax.random.split(key, 5)
        return {'input_ids': jax.random.randint(k[0], (B, S), 0, VOCAB, dtype=jnp.int64), 'emb_table': jax.random.normal(k[1], (VOCAB, D), dtype=jnp.float32), 'gate_table': jax.random.uniform(k[2], (VOCAB, 1), dtype=jnp.float32, minval=0.001, maxval=1.0), 'expert_w': jax.random.normal(k[3], (E, D, D), dtype=jnp.float32) * 0.02, 'expert_b': jax.random.normal(k[4], (E, D), dtype=jnp.float32) * 0.02}
    _L0_tok_all = _L0_tok_setup()
    _L0_tok_in = {k: v for k, v in _L0_tok_all.items() if k in ('emb_table', 'gate_table', 'expert_w', 'expert_b')}
    del _L0_tok_all

    def _L0_attn_setup():
        import jax, jax.numpy as jnp
        import numpy as np
        N_LAYERS = 2
        D = 128
        N = 16
        O = 128
        B = 4
        L = 512
        LN_EPS = 1e-05

        def _combine(e1, e2):
            a1, u1 = e1
            a2, u2 = e2
            return (a1 * a2, a2 * u1 + u2)
        key = jax.random.key(seed)
        ks = jax.random.split(key, 10)
        s = D ** (-0.5)
        inp = {'x': jax.random.normal(ks[0], (B, L, D), jnp.float32), 'A_log': jax.random.normal(ks[1], (N_LAYERS, D, N), jnp.float32) * 0.5, 'W_B': jax.random.normal(ks[2], (N_LAYERS, D, N), jnp.float32) * s, 'b_B': jnp.zeros((N_LAYERS, N), jnp.float32), 'W_C': jax.random.normal(ks[3], (N_LAYERS, D, N), jnp.float32) * s, 'b_C': jnp.zeros((N_LAYERS, N), jnp.float32), 'W_dt': jax.random.normal(ks[4], (N_LAYERS, D, D), jnp.float32) * s, 'b_dt': jnp.zeros((N_LAYERS, D), jnp.float32), 'D_skip': jnp.ones((N_LAYERS, D), jnp.float32), 'W_mix': jax.random.normal(ks[5], (N_LAYERS, D, D), jnp.float32) * s, 'b_mix': jnp.zeros((N_LAYERS, D), jnp.float32), 'ln_g': jnp.ones((N_LAYERS, D), jnp.float32), 'ln_b': jnp.zeros((N_LAYERS, D), jnp.float32), 'W_dec': jax.random.normal(ks[6], (D, O), jnp.float32) * s, 'b_dec': jnp.zeros((O,), jnp.float32)}
        return inp
    _L0_attn_all = _L0_attn_setup()
    _L0_attn_in = {k: v for k, v in _L0_attn_all.items() if k in ('A_log', 'W_B', 'b_B', 'W_C', 'b_C', 'W_dt', 'b_dt', 'D_skip', 'W_mix', 'b_mix', 'ln_g', 'ln_b', 'W_dec', 'b_dec')}
    del _L0_attn_all

    def _L0_ffn_setup():
        import jax, jax.numpy as jnp
        import numpy as np
        import math
        E, K, CAPF = (8, 2, 1.25)
        D, DFF = (128, 512)

        def _moe(x, Wr, br, W1, b1, W2, b2):
            orig = x.shape
            d = orig[-1]
            xf = x.reshape(-1, d)
            N = xf.shape[0]
            logits = xf @ Wr + br
            probs = jax.nn.softmax(logits, axis=-1)
            topk_p, topk_i = jax.lax.top_k(probs, K)
            topk_w = topk_p / (jnp.sum(topk_p, axis=-1, keepdims=True) + 1e-09)
            cap = max(1, int(math.ceil(CAPF * float(N * K) / float(E))))
            flat_e = topk_i.reshape(-1)
            flat_w = topk_w.reshape(-1)
            tok = jnp.repeat(jnp.arange(N), K)
            one_hot = jax.nn.one_hot(flat_e, E, dtype=xf.dtype)
            pos = (jnp.cumsum(one_hot, axis=0) - one_hot)[jnp.arange(N * K), flat_e]
            pos = pos.astype(jnp.int32)
            keep = pos < cap
            w_k = jnp.where(keep, flat_w, 0.0)
            sum_w = jnp.zeros((N,), xf.dtype).at[tok].add(w_k)
            w_norm = w_k / (sum_w[tok] + 1e-09)
            slot = flat_e * cap + pos
            slot_safe = jnp.where(keep, slot, E * cap)
            expert_in = jnp.zeros((E * cap, d), xf.dtype).at[slot_safe].set(xf[tok], mode='drop').reshape(E, cap, d)
            h = jax.nn.gelu(jnp.einsum('ecd,edf->ecf', expert_in, W1) + b1[:, None, :], approximate=False)
            expert_out = (jnp.einsum('ecf,efd->ecd', h, W2) + b2[:, None, :]).reshape(E * cap, d)
            contrib = expert_out[jnp.where(keep, slot, 0)]
            y = jnp.zeros((N, d), xf.dtype).at[tok].add(contrib * w_norm[:, None])
            return y.reshape(orig)
        key = jax.random.key(seed)
        ks = jax.random.split(key, 5)
        s = lambda k, sh, sc: jax.random.normal(k, sh, jnp.float32) * sc
        return {'x': jax.random.normal(ks[0], (8, 1024, D), jnp.float32), 'Wr': s(ks[1], (D, E), 1.0 / math.sqrt(D)), 'br': jnp.zeros((E,), jnp.float32), 'W1': s(ks[2], (E, D, DFF), 1.0 / math.sqrt(D)), 'b1': jnp.zeros((E, DFF), jnp.float32), 'W2': s(ks[3], (E, DFF, D), 1.0 / math.sqrt(DFF)), 'b2': jnp.zeros((E, D), jnp.float32)}
    _L0_ffn_all = _L0_ffn_setup()
    _L0_ffn_in = {k: v for k, v in _L0_ffn_all.items() if k in ('Wr', 'br', 'W1', 'b1', 'W2', 'b2')}
    del _L0_ffn_all
    return {'x': x, 'L0_tok_emb_table': _L0_tok_in['emb_table'], 'L0_tok_gate_table': _L0_tok_in['gate_table'], 'L0_tok_expert_w': _L0_tok_in['expert_w'], 'L0_tok_expert_b': _L0_tok_in['expert_b'], 'L0_attn_A_log': _L0_attn_in['A_log'], 'L0_attn_W_B': _L0_attn_in['W_B'], 'L0_attn_b_B': _L0_attn_in['b_B'], 'L0_attn_W_C': _L0_attn_in['W_C'], 'L0_attn_b_C': _L0_attn_in['b_C'], 'L0_attn_W_dt': _L0_attn_in['W_dt'], 'L0_attn_b_dt': _L0_attn_in['b_dt'], 'L0_attn_D_skip': _L0_attn_in['D_skip'], 'L0_attn_W_mix': _L0_attn_in['W_mix'], 'L0_attn_b_mix': _L0_attn_in['b_mix'], 'L0_attn_ln_g': _L0_attn_in['ln_g'], 'L0_attn_ln_b': _L0_attn_in['ln_b'], 'L0_attn_W_dec': _L0_attn_in['W_dec'], 'L0_attn_b_dec': _L0_attn_in['b_dec'], 'L0_ffn_Wr': _L0_ffn_in['Wr'], 'L0_ffn_br': _L0_ffn_in['br'], 'L0_ffn_W1': _L0_ffn_in['W1'], 'L0_ffn_b1': _L0_ffn_in['b1'], 'L0_ffn_W2': _L0_ffn_in['W2'], 'L0_ffn_b2': _L0_ffn_in['b2']}

def reference(x, L0_tok_emb_table, L0_tok_gate_table, L0_tok_expert_w, L0_tok_expert_b, L0_attn_A_log, L0_attn_W_B, L0_attn_b_B, L0_attn_W_C, L0_attn_b_C, L0_attn_W_dt, L0_attn_b_dt, L0_attn_D_skip, L0_attn_W_mix, L0_attn_b_mix, L0_attn_ln_g, L0_attn_ln_b, L0_attn_W_dec, L0_attn_b_dec, L0_ffn_Wr, L0_ffn_br, L0_ffn_W1, L0_ffn_b1, L0_ffn_W2, L0_ffn_b2):
    import jax
    import jax.numpy as jnp

    def _L0_tok_ref(input_ids, emb_table, gate_table, expert_w, expert_b):
        import jax, jax.numpy as jnp
        import numpy as np
        VOCAB, D, B, S, E = (50257, 128, 8, 512, 5)
        L_CONST = 1000000000.0
        d = emb_table.shape[1]
        n_exp = expert_w.shape[0]
        data = emb_table[input_ids]
        gate = gate_table[input_ids] * d
        idx_arr = jnp.arange(d, dtype=gate.dtype)
        frac = (L_CONST * gate - jnp.floor(L_CONST * gate)) / L_CONST
        mask = (idx_arr[None, None, :] < gate).astype(gate.dtype) + frac
        divisor = float(d // n_exp)
        eidx = jnp.clip(jnp.floor_divide(mask.sum(-1), divisor).astype(jnp.int32), 0, n_exp - 1)
        xm = data * mask
        y_all = jnp.einsum('bsd,eod->bseo', xm, expert_w) + expert_b[None, None]
        onehot = jax.nn.one_hot(eidx, n_exp, dtype=xm.dtype)
        return jnp.einsum('bseo,bse->bso', y_all, onehot)

    def _L0_attn_ref(x, A_log, W_B, b_B, W_C, b_C, W_dt, b_dt, D_skip, W_mix, b_mix, ln_g, ln_b, W_dec, b_dec):
        import jax, jax.numpy as jnp
        import numpy as np
        N_LAYERS = 2
        D = 128
        N = 16
        O = 128
        B = 4
        L = 512
        LN_EPS = 1e-05

        def _combine(e1, e2):
            a1, u1 = e1
            a2, u2 = e2
            return (a1 * a2, a2 * u1 + u2)
        h_in = x
        for i in range(N_LAYERS):
            A = -jnp.exp(A_log[i])
            Bm = h_in @ W_B[i] + b_B[i]
            Cm = h_in @ W_C[i] + b_C[i]
            dt = jax.nn.softplus(h_in @ W_dt[i] + b_dt[i])
            a = jnp.exp(dt[..., None] * A)
            u = (dt * h_in)[..., None] * Bm[:, :, None, :]
            _, h = jax.lax.associative_scan(_combine, (a, u), axis=1)
            y = jnp.einsum('bln,bldn->bld', Cm, h) + D_skip[i] * h_in
            y = jax.nn.gelu(y, approximate=False)
            y = y @ W_mix[i] + b_mix[i]
            mu = jnp.mean(y, axis=-1, keepdims=True)
            var = jnp.var(y, axis=-1, keepdims=True)
            y = (y - mu) / jnp.sqrt(var + LN_EPS) * ln_g[i] + ln_b[i]
            h_in = h_in + y
        return h_in @ W_dec + b_dec

    def _L0_ffn_ref(x, Wr, br, W1, b1, W2, b2):
        import jax, jax.numpy as jnp
        import numpy as np
        import math
        E, K, CAPF = (8, 2, 1.25)
        D, DFF = (128, 512)

        def _moe(x, Wr, br, W1, b1, W2, b2):
            orig = x.shape
            d = orig[-1]
            xf = x.reshape(-1, d)
            N = xf.shape[0]
            logits = xf @ Wr + br
            probs = jax.nn.softmax(logits, axis=-1)
            topk_p, topk_i = jax.lax.top_k(probs, K)
            topk_w = topk_p / (jnp.sum(topk_p, axis=-1, keepdims=True) + 1e-09)
            cap = max(1, int(math.ceil(CAPF * float(N * K) / float(E))))
            flat_e = topk_i.reshape(-1)
            flat_w = topk_w.reshape(-1)
            tok = jnp.repeat(jnp.arange(N), K)
            one_hot = jax.nn.one_hot(flat_e, E, dtype=xf.dtype)
            pos = (jnp.cumsum(one_hot, axis=0) - one_hot)[jnp.arange(N * K), flat_e]
            pos = pos.astype(jnp.int32)
            keep = pos < cap
            w_k = jnp.where(keep, flat_w, 0.0)
            sum_w = jnp.zeros((N,), xf.dtype).at[tok].add(w_k)
            w_norm = w_k / (sum_w[tok] + 1e-09)
            slot = flat_e * cap + pos
            slot_safe = jnp.where(keep, slot, E * cap)
            expert_in = jnp.zeros((E * cap, d), xf.dtype).at[slot_safe].set(xf[tok], mode='drop').reshape(E, cap, d)
            h = jax.nn.gelu(jnp.einsum('ecd,edf->ecf', expert_in, W1) + b1[:, None, :], approximate=False)
            expert_out = (jnp.einsum('ecf,efd->ecd', h, W2) + b2[:, None, :]).reshape(E * cap, d)
            contrib = expert_out[jnp.where(keep, slot, 0)]
            y = jnp.zeros((N, d), xf.dtype).at[tok].add(contrib * w_norm[:, None])
            return y.reshape(orig)
        return _moe(x, Wr, br, W1, b1, W2, b2)
    h = _L0_tok_ref(x, L0_tok_emb_table, L0_tok_gate_table, L0_tok_expert_w, L0_tok_expert_b)
    h = h + _L0_attn_ref(_layernorm(h, axis=-1), L0_attn_A_log, L0_attn_W_B, L0_attn_b_B, L0_attn_W_C, L0_attn_b_C, L0_attn_W_dt, L0_attn_b_dt, L0_attn_D_skip, L0_attn_W_mix, L0_attn_b_mix, L0_attn_ln_g, L0_attn_ln_b, L0_attn_W_dec, L0_attn_b_dec)
    h = h + _L0_ffn_ref(_layernorm(h, axis=-1), L0_ffn_Wr, L0_ffn_br, L0_ffn_W1, L0_ffn_b1, L0_ffn_W2, L0_ffn_b2)
    return h

_drawn_inputs = setup_inputs


def setup_inputs(seed=0):
    import zlib

    import numpy as np

    out = dict(_drawn_inputs(seed))
    spreads = {'L0_attn_b_B': (0.0, 0.1),
     'L0_attn_b_C': (0.0, 0.1),
     'L0_attn_b_dt': (0.0, 0.1),
     'L0_attn_D_skip': (1.0, 0.2),
     'L0_attn_b_mix': (0.0, 0.1),
     'L0_attn_ln_g': (1.0, 0.2),
     'L0_attn_ln_b': (0.0, 0.1),
     'L0_attn_b_dec': (0.0, 0.1),
     'L0_ffn_br': (0.0, 0.1),
     'L0_ffn_b1': (0.0, 0.285),
     'L0_ffn_b2': (0.0, 0.1)}
    factors = {}
    for name, (base, spread) in spreads.items():
        noise = np.random.default_rng([zlib.crc32(name.encode()), seed]).standard_normal(out[name].shape)
        drawn = base * np.exp(spread * noise) if base else spread * noise
        out[name] = jnp.asarray(drawn.astype(out[name].dtype))
    for name, factor in factors.items():
        out[name] = (out[name] * factor).astype(out[name].dtype)
    return out
```

```python
import concourse.bass as bass
from concourse import mybir
from contextlib import ExitStack

F32, BF16 = mybir.dt.float32, mybir.dt.bfloat16
I32, U32 = mybir.dt.int32, mybir.dt.uint32
ALU = mybir.AluOpType
ACT = mybir.ActivationFunctionType
AX = mybir.AxisListType


class Chain:

    def __init__(self, engine, semaphore):
        self.engine, self.semaphore, self.count = engine, semaphore, 0

    def mark(self, instruction):
        instruction.then_inc(self.semaphore, 1)
        self.count += 1
        return self.count

    def need(self, count):
        self.engine.wait_ge(self.semaphore, count)

    def link(self, instruction):
        self.need(self.mark(instruction))


def tower_kernel(nc, ids, emb_table, gate_table, tok_w, tok_b, A_log, W_B, b_B, W_C, b_C, W_dt, b_dt,
                 D_skip, W_mix, b_mix, ln_g, ln_b, W_dec, b_dec, Wr, br, W1, b1, W2, b2, out):
    P = 128
    VOCAB, D = emb_table.shape
    NT = ids.shape[1]
    T = NT * P
    NSEQ, L = 2, T // 2
    NL = A_log.shape[1]
    NS = A_log.shape[2]
    ET = tok_w.shape[1]
    NE = Wr.shape[1]
    FF = W1.shape[2]
    FC = FF // P
    TOPK = 2
    CAP = -(-5 * T * TOPK // (4 * NE))
    ROWS = NE * CAP
    ST = CAP // P
    HALF = 512
    TPG = HALF // D
    NG = NT // TPG
    NPH = NL * NSEQ
    GU = 4
    NQ = NS // GU
    EPS = 1e-5
    STEP = D // ET
    EXACT = float(2 ** 23)
    N_LOADS = 16
    assert ROWS % P == 0 and CAP % P == 0 and NS == 16

    x_rows = nc.dram_tensor("x_rows", [ROWS, D], F32, kind="Internal").ap()
    y_rows = nc.dram_tensor("y_rows", [ROWS, D], F32, kind="Internal").ap()
    c_dram = nc.dram_tensor("c_dram", [NPH, NS, L], F32, kind="Internal").ap()

    ctx = ExitStack()
    with ctx:
        def sb(name, shape, dt=F32):
            return ctx.enter_context(nc.sbuf_tensor(name, shape, dt))

        def sem(name):
            return ctx.enter_context(nc.semaphore(name))

        ident = sb("ident", [P, P])
        iota_d = sb("iota_d", [P, P])
        sel = sb("sel", [P, NS, P], BF16)
        tri = sb("tri", [P, P], BF16)
        ones_bf = sb("ones_bf", [P, P], BF16)
        mean_w = sb("mean_w", [P, P])
        iota_e = sb("iota_e", [P, NE])
        iota_cap = sb("iota_cap", [P, NE])
        not_first = sb("not_first", [P, NE, NT])
        eps_col = sb("eps_col", [P, 1])
        one_col = sb("one_col", [P, 1])
        tokw = sb("tokw", [P, ET, D])
        tokb_rep = sb("tokb_rep", [ET * 8, D])
        tokb_sel = sb("tokb_sel", [ET * 8, 8, D])
        negA = sb("negA", [P, NL, NS])
        wbc = sb("wbc", [P, NL, P])
        bbc = sb("bbc", [P, NL])
        wdt = sb("wdt", [P, NL, D])
        wmix = sb("wmix", [P, NL, D])
        cols = sb("cols", [P, 5, NL])
        dskip = sb("dskip", [P, NL, D])
        wdec = sb("wdec", [P, D])
        bdec_bc = sb("bdec_bc", [P, D])
        wr = sb("wr", [P, NE])
        br_bc = sb("br_bc", [P, NE])
        b1_sb = sb("b1_sb", [P, NE, FC])
        b2_bc = sb("b2_bc", [P, NE, D])
        ids_sb = sb("ids_sb", [P, NT], I32)
        idf = sb("idf", [P, 2, NT])
        idx = sb("idx", [P, NT], U32)
        gate = sb("gate", [P, 7, NT])
        gate_i = sb("gate_i", [P, NT], I32)
        ge = sb("ge", [P, NT, ET - 1])
        oh = sb("oh", [P, NT, ET])
        ohT = sb("ohT", [ET * 8, P])
        tok = sb("tok", [P, NT, D])
        stats = sb("stats", [P, NT, 6])
        mv = sb("mv", [P, NT, 2])
        rstd = sb("rstd", [P, 2, NT])
        z = sb("z", [P, NT, D])
        hT = [sb(f"hT{i}", [P, T]) for i in range(2)]
        dt = sb("dt", [P, 2, L])
        du = sb("du", [P, 2, L])
        bc = sb("bc", [P, L])
        rest = sb("rest", [96, L])
        part = sb("part", [96, L], BF16)
        split = [sb(f"split{i}", [96, L], BF16) for i in range(2)]
        a_ring = sb("a_ring", [P, GU, L])
        h_ring = sb("h_ring", [P, 2, L])
        g_ring = sb("g_ring", [P, 2, L])
        work = sb("work", [P, 2, L])
        big = sb("big", [P, NS, L])
        out_sb = h_ring[:, :, :].rearrange("p a b -> p (a b)").rearrange("p (j d) -> p j d", d=D)

        ps = ctx.enter_context(nc.psum_tensor("ps", [P, 8 * HALF], F32))

        def bank(i, n=1):
            return ps[:, i * HALF:(i + n) * HALF]

        emb = big[:, 0:2, :].rearrange("p a b -> p (a b)").rearrange("p (j d) -> p j d", d=D)
        xm = big[:, 2, 0:HALF].rearrange("p (q d) -> p q d", d=D)
        mk = big[:, 2, HALF:2 * HALF].rearrange("p (q d) -> p q d", d=D)
        xT = big[:, 3, 0:HALF]
        zero = big[:, 4:14, :].rearrange("p a b -> p (a b)")[:, 0:ROWS * D // P]
        flat = big[:, :, :].rearrange("p a b -> p (a b)")
        w1b = [flat[:, i * FF:(i + 1) * FF] for i in range(2)]
        w2b = [flat[:, (2 + i) * FF:(3 + i) * FF].rearrange("p (c d) -> p c d", d=D) for i in range(2)]
        o0 = 4 * FF
        xb = [flat[:, o0 + i * CAP:o0 + (i + 1) * CAP].rearrange("p (t d) -> p t d", d=D) for i in range(2)]
        xeT = [flat[:, o0 + (2 + i) * CAP:o0 + (3 + i) * CAP] for i in range(2)]
        ob = [flat[:, o0 + (4 + i) * CAP:o0 + (5 + i) * CAP].rearrange("p (t d) -> p t d", d=D) for i in range(2)]
        o1 = o0 + 6 * CAP
        hid = flat[:, o1:o1 + FC * CAP].rearrange("p (f c) -> p f c", f=FC)
        picked = [a_ring[:, 2 * k:2 * k + 2, :].rearrange("p a b -> p (a b)").rearrange("p (j d) -> p j d", d=D)
                  for k in range(TOPK)]
        lg = sb("lg", [P, NT, NE])
        pr = sb("pr", [P, NT, NE])
        rmax = sb("rmax", [P, 4, NT])
        m8 = sb("m8", [P, NT, 8])
        i8 = sb("i8", [P, NT, 8], U32)
        i8f = sb("i8f", [P, NT, TOPK])
        ohk = [sb(f"ohk{k}", [P, NT, NE]) for k in range(TOPK)]
        routed = sb("routed", [P, NT, NE], BF16)
        cnt = sb("cnt", [P, NE, NT])
        cum = sb("cum", [P, NE, NT])
        pos = sb("pos", [P, NT, NE])
        slot = sb("slot", [P, NT, NE])
        tmp = sb("tmp", [P, NT, NE])
        wk = sb("wk", [P, TOPK, NT])
        posk = sb("posk", [P, TOPK, NT])
        keep = sb("keep", [P, TOPK, NT])
        slotk = sb("slotk", [P, TOPK, NT])
        into = sb("into", [P, TOPK, NT], U32)
        outof = sb("outof", [P, TOPK, NT], U32)

        (ids_in, weights_in, wbc_in, wbc_zero, idx_ready, consts_ready, zero_ready, zeroed, negA_ready,
         mean_ready, bmix_mean, folded, masked, xT_ready, xT_copied, oh_ready, ohT_ready, ohT_copied, bias_ready,
         bias_copied, y_tok_ready, combined, var_ready, rstd_ready, z_ready, zT_ready, hT_ready,
         dt_psum, dt_parts, dt_ready, bc_psum, bc_ready, c_stored, split_first, split_second, split_ready,
         b_ready, a_ready, u_done, scanned, g_ready, y_added, y_ready, gelu_done, mixed, squared, var_psum,
         rstd_psum, z_psum, z_scaled, h_next, bdec_added, dec_psum, tok_done, var2_ready, rstd2_ready, z2_ready,
         z2T_ready, z2T_copied, logits_ready, shifted, exped, counted, pos_ready, idx_made, scattered,
         xeT_ready, xeT_copied, hid_psum, hid_ready, out_psum, out_copied, out_ready, out_stored,
         chain_dve, chain_pool, chain_act) = [sem(name) for name in """
            ids_in weights_in wbc_in wbc_zero idx_ready consts_ready zero_ready zeroed negA_ready
            mean_ready bmix_mean folded masked xT_ready xT_copied oh_ready ohT_ready ohT_copied bias_ready
            bias_copied y_tok_ready combined var_ready rstd_ready z_ready zT_ready hT_ready
            dt_psum dt_parts dt_ready bc_psum bc_ready c_stored split_first split_second split_ready
            b_ready a_ready u_done scanned g_ready y_added y_ready gelu_done mixed squared var_psum
            rstd_psum z_psum z_scaled h_next bdec_added dec_psum tok_done var2_ready rstd2_ready z2_ready
            z2T_ready z2T_copied logits_ready shifted exped counted pos_ready idx_made scattered
            xeT_ready xeT_copied hid_psum hid_ready out_psum out_copied out_ready out_stored
            chain_dve chain_pool chain_act""".split()]
        gate_in = [sem(f"gate_in{i}") for i in range(NSEQ)]
        emb_in = [sem(f"emb_in{i}") for i in range(NSEQ)]
        c_in = [sem(f"c_in{q}") for q in range(NQ)]
        w_in = [sem(f"w_in{i}") for i in range(2)]
        rows_in = [sem(f"rows_in{i}") for i in range(2)]
        rows_out = [sem(f"rows_out{i}") for i in range(2)]
        got = [sem(f"got{g}") for g in range(NG)]
        block = ctx.enter_context(nc.Block())

        def halves(ap):
            return [ap[:, h * HALF:(h + 1) * HALF] for h in range(2)]


        def tokens(p):
            return slice((p % NSEQ) * L, (p % NSEQ + 1) * L)

        def h_in(p):
            return hT[p // NSEQ % 2][:, tokens(p)]

        def h_out(p):
            return hT[(p // NSEQ + 1) % 2][:, tokens(p)]

        def pairs_of(engine, pieces, pair):
            for q in range(NQ):
                if 2 * q in pieces:
                    for k in (2 * q, 2 * q + 1):
                        pair(2 * k, q, 2 * k - GU * q)
                        if k in pieces:
                            pieces[k]()
                else:
                    with engine.Fori(0, GU // 2) as i:
                        pair(2 * i + GU * q, q, 2 * i)
                    if 2 * q + 1 in pieces:
                        pieces[2 * q + 1]()

        H_RING, A_RING, G_RING = 2, GU, 2
        HID_RING, OUT_RING = 2, 1
        N_BIG = 5
        W_PSUM = bank(6, 2)
        Y_PSUM = bank(4, 2)

        @block.sync
        def _(sp):
            sp.dma_start(ids_sb[:, :], ids).then_inc(ids_in, 16)
            loads = [(tokw[:, :, :], tok_w), (negA[:, :, :], A_log), (wdt[:, :, :], W_dt), (wmix[:, :, :], W_mix),
                     (wdec[:, :], W_dec), (wr[:, :], Wr), (b1_sb[:, :, :], b1), (tokb_rep[:, :], tok_b),
                     (bdec_bc[:, :], b_dec.broadcast_to([P, D])), (br_bc[:, :], br.broadcast_to([P, NE])),
                     (b2_bc[:, :, :], b2.broadcast_to([P, NE, D]))]
            loads += [(cols[:, i, :], c) for i, c in enumerate((b_dt, D_skip, b_mix, ln_g, ln_b))]
            assert len(loads) == N_LOADS
            for dst, src in loads:
                sp.dma_start(dst, src).then_inc(weights_in, 16)
            sp.wait_ge(wbc_zero, 2)
            for i, (w, b) in enumerate(((W_B, b_B), (W_B, b_B), (W_B, b_B), (W_C, b_C))):
                sp.dma_start(wbc[:, :, 32 * i:32 * i + NS], w).then_inc(wbc_in, 16)
                sp.dma_start(bbc[32 * i:32 * i + NS, :], b).then_inc(wbc_in, 16)
            sp.wait_ge(zero_ready, 1)
            sp.dma_start(x_rows.rearrange("(p n) d -> p (n d)", p=P), zero).then_inc(zeroed, 16)
            for p in range(NPH):
                sp.wait_ge(bc_ready, 2 * (p + 1))
                sp.dma_start(c_dram[p, :, :], bc[96:96 + NS, :]).then_inc(c_stored, 16)
                sp.wait_ge(c_stored, 16 * (p + 1))
                if p == 0:
                    sp.wait_ge(hT_ready, NG)
                    sp.wait_ge(zeroed, 16)
                for q in range(NQ):
                    if p > 0:
                        sp.wait_ge(g_ready, H_RING + NS * (p - 1) + GU * (q + 1))
                    sp.dma_start(big[:, GU * q:GU * (q + 1), :],
                                 c_dram[p:p + 1, GU * q:GU * (q + 1), :].broadcast_to([P, GU, L]))\
                        .then_inc(c_in[q], 16)

            w1_v = W1.rearrange("d e f -> d e f")
            rows_v = x_rows.rearrange("(e t p) d -> p e t d", p=P, e=NE)
            out_v = y_rows.rearrange("(e t p) d -> p e t d", p=P, e=NE)

            def load_weights(e, i):
                sp.dma_start(w1b[i], w1_v[:, e, :]).then_inc(w_in[i], 16)
                sp.dma_start(w2b[i].rearrange("p c d -> p (c d)"), W2[:, e, :]).then_inc(w_in[i], 16)

            def load_rows(e, i):
                sp.dma_start(xb[i], rows_v[:, e, :, :]).then_inc(rows_in[i], 16)

            def store_rows(e, i):
                sp.wait_ge(out_copied, OUT_RING + e + 1)
                sp.dma_start(out_v[:, e, :, :], ob[i]).then_inc(rows_out[i], 16)

            sp.wait_ge(g_ready, H_RING + NS * NPH)
            for i in range(2):
                sp.sem_inc(rows_out[i], 16)
                load_weights(i, i)
            sp.wait_ge(scattered, 16 * TOPK * NT)
            for i in range(2):
                load_rows(i, i)
            with sp.Fori(0, NE // 2 - 1) as k:
                for i in range(2):
                    e = 2 * k
                    sp.wait_ge(out_psum, e + i + 1)
                    load_weights(e + i + 2, i)
                    load_rows(e + i + 2, i)
                    store_rows(e + i, i)
            for i in range(2):
                store_rows(NE - 2 + i, i)
            for h in range(NSEQ):
                sp.wait_ge(out_ready, NT // NSEQ * (h + 1))
                js = slice(h * NT // NSEQ, (h + 1) * NT // NSEQ)
                sp.dma_start(out[:, js, :], out_sb[:, js, :]).then_inc(out_stored, 16)
            sp.wait_ge(out_stored, 16 * NSEQ)

        @block.gpsimd
        def _(pool):
            v = nc.gpsimd
            own = Chain(pool, chain_pool)
            v.memset(wbc[:, :, :], 0.0).then_inc(wbc_zero, 1)
            v.memset(bbc[:, :], 0.0).then_inc(wbc_zero, 1)
            v.iota(iota_d[:, :], [[1, P]], 0, 0, allow_small_or_imprecise_dtypes=True)
            own.link(v.memset(ident[:, :], 0.0))
            own.link(v.affine_select(ident[:, :], ident[:, :], [[-1, P]], ALU.not_equal, 1.0, 0, 1))
            pool.wait_ge(idx_ready, 1)
            for h in range(NSEQ):
                for j in range(h * NT // NSEQ, (h + 1) * NT // NSEQ):
                    v.indirect_dma_start(gate[:, 0, j:j + 1], None, gate_table,
                                         bass.IndirectOffsetOnAxis(ap=idx[:, j:j + 1], axis=0)).then_inc(gate_in[h], 16)
                for j in range(h * NT // NSEQ, (h + 1) * NT // NSEQ):
                    v.indirect_dma_start(emb[:, j, :], None, emb_table,
                                         bass.IndirectOffsetOnAxis(ap=idx[:, j:j + 1], axis=0)).then_inc(emb_in[h], 16)
            pool.wait_ge(weights_in, 16 * N_LOADS)
            own.link(v.affine_select(tokb_sel[:, :, :], tokb_rep[:, None, :].broadcast_to([ET * 8, 8, D]),
                                     [[-ET, 8], [0, D]], ALU.is_ge, 0.0, 0, 1))
            own.link(v.affine_select(tokb_sel[:, :, :], tokb_sel[:, :, :],
                                     [[ET, 8], [0, D]], ALU.is_ge, 0.0, ET - 1, -1))
            v.memset(zero, 0.0).then_inc(zero_ready, 1)
            v.memset(mean_w[:, :], 1.0 / D)
            own.link(v.memset(sel[:, :, :], 0.0))
            for k in range(3):
                own.link(v.affine_select(sel[:, :, :], sel[:, :, :], [[-1, NS], [0, P]], ALU.not_equal, 1.0,
                                         -32 * k, 1))
            own.link(v.memset(ones_bf[:, :], 1.0))
            own.link(v.affine_select(tri[:, :], ones_bf[:, :], [[1, P]], ALU.is_gt, 0.0, 0, -1))
            v.iota(iota_e[:, :], [[1, NE]], 0, 0, allow_small_or_imprecise_dtypes=True)
            v.iota(iota_cap[:, :], [[CAP, NE]], 0, 0, allow_small_or_imprecise_dtypes=True)
            own.link(v.memset(not_first[:, :, :], 1.0))
            v.memset(not_first[:, :, 0:1], 0.0).then_inc(consts_ready, 1)

            def step_size(p):
                pool.wait_ge(dt_parts, p + 1)
                own.link(v.tensor_tensor(dt[:, p % 2, :], work[:, 0, :], work[:, 1, :], ALU.add))
                v.tensor_tensor(du[:, p % 2, :], dt[:, p % 2, :], h_in(p), ALU.mult).then_inc(dt_ready, 1)

            pool.sem_inc(g_ready, H_RING)
            step_size(0)
            for p in range(NPH):
                def pair(n, q, i):
                    for r in range(2):
                        u = NS * p + n + r
                        pool.wait_ge(scanned, A_RING + u + 1)
                        pool.wait_ge(y_added, u + 1)
                        v.tensor_tensor(g_ring[:, r, :], h_ring[:, r, :], big[:, n + r, :], ALU.mult)\
                            .then_inc(g_ready, 1)

                pieces = {5: lambda: step_size(p + 1)} if p + 1 < NPH else {}
                for q in range(NQ):
                    pool.wait_ge(c_in[q], 16 * (p + 1))
                    if 2 * q in pieces or 2 * q + 1 in pieces:
                        for k in (2 * q, 2 * q + 1):
                            pair(2 * k, q, 0)
                            if k in pieces:
                                pieces[k]()
                    else:
                        with pool.Fori(0, GU // 2) as i:
                            pair(2 * i + GU * q, q, 2 * i)
            pool.wait_ge(zeroed, 16)
            pool.wait_ge(idx_made, 2)
            for k in range(TOPK):
                for j in range(NT):
                    v.indirect_dma_start(x_rows, bass.IndirectOffsetOnAxis(ap=into[:, k, j:j + 1], axis=0),
                                         z[:, j, :], None, bounds_check=ROWS - 1, oob_is_err=False)\
                        .then_inc(scattered, 16)
            for i in range(2):
                pool.wait_ge(rows_out[i], 16 + 16 * NE // 2)
            for j in range(NT):
                for k in range(TOPK):
                    v.indirect_dma_start(picked[k][:, j, :], None, y_rows,
                                         bass.IndirectOffsetOnAxis(ap=outof[:, k, j:j + 1], axis=0))\
                        .then_inc(got[j // TPG], 16)

        @block.scalar
        def _(act):
            v = nc.scalar
            own = Chain(act, chain_act)
            v.preload_act_table_set("natural_log_exp_and_others")
            act.wait_ge(weights_in, 16 * N_LOADS)
            own.link(v.activation(negA[:, :, :], negA[:, :, :], ACT.Exp))
            v.activation(negA[:, :, :], negA[:, :, :], ACT.Copy, scale=-1.0).then_inc(negA_ready, 1)

            def reciprocal_root(dst, var, tmp):
                own.link(v.activation(tmp, var, ACT.Ln, bias=eps_col[:, :]))
                return v.activation(dst, tmp, ACT.Exp, scale=-0.5)

            act.wait_ge(mean_ready, 1)
            for g in range(NG):
                act.wait_ge(xT_ready, g + 1)
                v.activation(xT, bank(0), ACT.Copy).then_inc(xT_copied, 1)
                if g % 2 == 0:
                    act.wait_ge(ohT_ready, g // 2 + 1)
                    v.activation(ohT[:, :], bank(7)[0:ET * 8, 0:P], ACT.Copy).then_inc(ohT_copied, 1)
                act.wait_ge(bias_ready, g + 1)
                v.activation(tok[:, TPG * g:TPG * (g + 1), :], bank(7).rearrange("p (q d) -> p q d", d=D), ACT.Copy)\
                    .then_inc(bias_copied, 1)
                act.wait_ge(var_ready, g + 1)
                js = slice(TPG * g, TPG * (g + 1))
                reciprocal_root(rstd[:, 0, js], mv[:, js, 1], rstd[:, 1, js]).then_inc(rstd_ready, 1)
                act.wait_ge(zT_ready, g + 1)
                v.activation(hT[0][:, HALF * g:HALF * (g + 1)], bank(7), ACT.Copy).then_inc(hT_ready, 1)

            def softplus_parts(p):
                l = p // NSEQ
                act.wait_ge(dt_psum, p + 1)
                own.link(v.activation(work[:, 0, :], W_PSUM, ACT.Abs, bias=cols[:, 0, l:l + 1]))
                v.activation(work[:, 1, :], W_PSUM, ACT.Relu, bias=cols[:, 0, l:l + 1]).then_inc(chain_act, 1)
                own.count += 1
                own.link(v.activation(work[:, 0, :], work[:, 0, :], ACT.Exp, scale=-1.0))
                v.activation(work[:, 0, :], work[:, 0, :], ACT.Ln, bias=one_col[:, :]).then_inc(dt_parts, 1)

            def b_and_c(p):
                l = p // NSEQ
                act.wait_ge(bc_psum, p + 1)
                if p > 0:
                    act.wait_ge(c_stored, 16 * p)
                    act.wait_ge(split_ready, p)
                v.activation(bc[:, :], W_PSUM, ACT.Identity, bias=bbc[:, l:l + 1]).then_inc(bc_ready, 1)
                v.activation(split[p % 2][:, :], W_PSUM[0:96, :], ACT.Identity, bias=bbc[0:96, l:l + 1])\
                    .then_inc(bc_ready, 1)

            def second_part(p):
                act.wait_ge(split_first, p + 1)
                v.activation(part[:, :], rest[:, :], ACT.Copy).then_inc(split_second, 1)

            def gelu(p):
                act.wait_ge(y_ready, p + 1)
                v.activation(work[:, 0, :], Y_PSUM, ACT.Gelu).then_inc(gelu_done, 1)
                v.preload_act_table_set("natural_log_exp_and_others")

            def centre(p):
                l = p // NSEQ
                act.wait_ge(mixed, p + 1)
                v.activation(work[:, 1, :], W_PSUM, ACT.Identity, bias=cols[:, 2, l:l + 1]).then_inc(chain_act, 1)
                own.count += 1
                v.activation(work[:, 0, :], W_PSUM, ACT.Square, bias=cols[:, 2, l:l + 1]).then_inc(squared, 1)

            def root(p):
                act.wait_ge(var_psum, p + 1)
                reciprocal_root(W_PSUM, W_PSUM, W_PSUM).then_inc(rstd_psum, 1)

            def scale_norm(p):
                l = p // NSEQ
                act.wait_ge(z_psum, p + 1)
                v.activation(W_PSUM, W_PSUM, ACT.Identity, bias=cols[:, 4, l:l + 1], scale=cols[:, 3, l:l + 1])\
                    .then_inc(z_scaled, 1)

            softplus_parts(0)
            b_and_c(0)
            second_part(0)
            for p in range(NPH):
                def pair(n, q, i):
                    for r in range(2):
                        u = NS * p + n + r
                        act.wait_ge(scanned, u + 1)
                        nn = n + r
                        v.activation(a_ring[:, i + r, :], dt[:, p % 2, :], ACT.Exp,
                                     scale=negA[:, p // NSEQ, bass.ds(nn, 1)]).then_inc(a_ready, 1)

                act.wait_ge(dt_ready, p + 1)
                pieces = {}
                if p > 0:
                    pieces[1] = lambda: gelu(p - 1)
                    pieces[2] = lambda: (centre(p - 1), root(p - 1))
                    pieces[3] = lambda: scale_norm(p - 1)
                if p + 1 < NPH:
                    pieces[4] = lambda: softplus_parts(p + 1)
                    pieces[5] = lambda: b_and_c(p + 1)
                    pieces[6] = lambda: second_part(p + 1)
                pairs_of(act, pieces, pair)
            last = NPH - 1
            gelu(last)
            centre(last)
            root(last)
            scale_norm(last)
            for g in range(NG):
                js = slice(TPG * g, TPG * (g + 1))
                act.wait_ge(var2_ready, g + 1)
                reciprocal_root(rstd[:, 0, js], mv[:, js, 1], rstd[:, 1, js]).then_inc(rstd2_ready, 1)
                act.wait_ge(z2T_ready, g + 1)
                v.activation(work[:, g % 2, 0:HALF], bank(2 + g % 2), ACT.Copy).then_inc(z2T_copied, 1)
            act.wait_ge(shifted, 1)
            v.activation(pr[:, :, :], lg[:, :, :], ACT.Exp).then_inc(exped, 1)
            act.sem_inc(hid_ready, HID_RING)
            with act.Fori(0, NE) as e:
                for f in range(FC):
                    act.wait_ge(hid_psum, FC * e + f + 1)
                    v.activation(hid[:, f, :].rearrange("p (a b) -> p a b", a=2),
                                 bank(2 * (f % 2), 2).rearrange("p (a b) -> p a b", a=2)[:, :, 0:CAP // 2],
                                 ACT.Gelu, bias=b1_sb[:, e, f:f + 1]).then_inc(hid_ready, 1)

        @block.vector
        def _(dve):
            v = nc.vector
            own = Chain(dve, chain_dve)
            v.memset(eps_col[:, :], EPS)
            v.memset(one_col[:, :], 1.0)
            dve.wait_ge(ids_in, 16)
            own.link(v.tensor_copy(idf[:, 0, :], ids_sb[:, :]))
            own.link(v.tensor_scalar(idf[:, 1, :], idf[:, 0, :], 0.0, float(VOCAB), ALU.is_lt, ALU.mult))
            own.link(v.tensor_tensor(idf[:, 0, :], idf[:, 0, :], idf[:, 1, :], ALU.add))
            own.link(v.tensor_scalar(idf[:, 0, :], idf[:, 0, :], 0.0, float(VOCAB - 1), ALU.max, ALU.min))
            v.tensor_copy(idx[:, :], idf[:, 0, :]).then_inc(idx_ready, 1)
            dve.wait_ge(weights_in, 16 * N_LOADS)
            dve.wait_ge(zero_ready, 1)
            own.link(v.tensor_reduce(idf[:, 0, 0:NL], wmix[:, :, :], AX.X, ALU.add))
            own.link(v.tensor_scalar(idf[:, 0, 0:NL], idf[:, 0, 0:NL], 1.0 / D, None, ALU.mult))
            for l in range(NL):
                own.link(v.tensor_scalar(wmix[:, l, :], wmix[:, l, :], idf[:, 0, l:l + 1], None, ALU.subtract))
                own.link(v.tensor_scalar(dskip[:, l, :], ident[:, :], cols[:, 1, l:l + 1], None, ALU.mult))
            dve.wait_ge(consts_ready, 1)
            dve.wait_ge(bmix_mean, 1)
            own.link(v.tensor_tensor(cols[:, 2, :], cols[:, 2, :], bank(0)[:, 0:NL], ALU.subtract))
            v.tensor_copy(idf[:, 1, 0:1], idf[:, 0, 0:1]).then_inc(mean_ready, 1)

            def gates(h):
                js = slice(h * NT // NSEQ, (h + 1) * NT // NSEQ)
                n = NT // NSEQ
                raw, g, c, fl, ab, fr = [gate[:, i, js] for i in range(6)]
                dve.wait_ge(gate_in[h], 16 * n)
                own.link(v.tensor_scalar(g, raw, float(D), None, ALU.mult))
                own.link(v.tensor_scalar(c, g, 1e9, None, ALU.mult))
                own.link(v.tensor_scalar(c, c, -EXACT, EXACT, ALU.max, ALU.min))
                own.link(v.tensor_copy(gate_i[:, js], c))
                own.link(v.tensor_copy(fl, gate_i[:, js]))
                own.link(v.tensor_tensor(ab, fl, c, ALU.is_gt))
                own.link(v.tensor_tensor(fl, fl, ab, ALU.subtract))
                own.link(v.tensor_tensor(fr, c, fl, ALU.subtract))
                own.link(v.tensor_scalar(fr, fr, 1e-9, None, ALU.mult))
                for k in range(1, ET):
                    own.link(v.tensor_scalar(ge[:, js, k - 1], g, float(k * STEP - 1), None, ALU.is_gt))
                own.link(v.tensor_scalar(oh[:, js, 0], ge[:, js, 0], -1.0, 1.0, ALU.mult, ALU.add))
                for k in range(1, ET - 1):
                    own.link(v.tensor_tensor(oh[:, js, k], ge[:, js, k - 1], ge[:, js, k], ALU.subtract))
                v.tensor_copy(oh[:, js, ET - 1], ge[:, js, ET - 2]).then_inc(oh_ready, 1)
                dve.wait_ge(oh_ready, h + 1)

            def mask(g):
                if g > 0:
                    dve.wait_ge(xT_ready, g)
                for q in range(TPG):
                    j = TPG * g + q
                    n = own.mark(v.tensor_scalar(mk[:, q, :], iota_d[:, :], gate[:, 1, j:j + 1],
                                                 gate[:, 5, j:j + 1], ALU.is_lt, ALU.add))
                own.need(n)
                for q in range(TPG):
                    last = v.tensor_tensor(xm[:, q, :], emb[:, TPG * g + q, :], mk[:, q, :], ALU.mult)
                last.then_inc(masked, 1)

            def normalise(g, ready):
                dve.wait_ge(ready, g + 1)
                for j in range(TPG * g, TPG * (g + 1)):
                    last = v.tensor_scalar(z[:, j, :], tok[:, j, :], mv[:, j, 0:1], rstd[:, 0, j:j + 1],
                                           ALU.subtract, ALU.mult)
                return last

            def moments(g):
                for j in range(TPG * g, TPG * (g + 1)):
                    n = own.mark(v.bn_stats(stats[:, j, :], tok[:, j, :]))
                own.need(n)
                for j in range(TPG * g, TPG * (g + 1)):
                    last = v.bn_aggr(mv[:, j, :], stats[:, j, :])
                return last

            for g in range(NG):
                if g % 2 == 0:
                    gates(g // 2)
                    dve.wait_ge(emb_in[g // 2], 16 * NT // NSEQ)
                mask(g)
                dve.wait_ge(bias_copied, g + 1)
                for pr_ in range(2):
                    dve.wait_ge(y_tok_ready, 2 * g + pr_ + 1)
                    b0 = 1 + 3 * pr_
                    done = [0, 0]
                    for e in range(ET):
                        for r in range(2):
                            j = TPG * g + 2 * pr_ + r
                            y = bank(b0 + r)[:, e * D:(e + 1) * D] if e < 4 else bank(b0 + 2)[:, r * D:(r + 1) * D]
                            if e:
                                own.need(done[r])
                            done[r] = own.mark(v.scalar_tensor_tensor(tok[:, j, :], y, oh[:, j, e:e + 1], tok[:, j, :],
                                                                      ALU.mult, ALU.add))
                    own.need(done[1])
                    v.memset(idf[:, 1, 0:1], 0.0).then_inc(combined, 1)
                moments(g).then_inc(var_ready, 1)
                normalise(g, rstd_ready).then_inc(z_ready, 1)

            def first_rest(p):
                dve.wait_ge(bc_ready, 2 * (p + 1))
                v.tensor_tensor(rest[:, :], bc[0:96, :], split[p % 2][:, :], ALU.subtract).then_inc(split_first, 1)

            def second_rest(p):
                dve.wait_ge(split_second, p + 1)
                v.tensor_copy(split[p % 2][32:64, :], part[32:64, :])
                own.link(v.tensor_tensor(rest[:, :], rest[:, :], part[:, :], ALU.subtract))
                v.tensor_copy(split[p % 2][64:96, :], rest[64:96, :]).then_inc(split_ready, 1)

            def normed(p):
                dve.wait_ge(rstd_psum, p + 1)
                v.tensor_tensor(W_PSUM, work[:, 1, :], W_PSUM, ALU.mult).then_inc(z_psum, 1)

            def residual(p):
                dve.wait_ge(z_scaled, p + 1)
                v.tensor_tensor(h_out(p), W_PSUM, h_in(p), ALU.add).then_inc(h_next, 1)

            dve.sem_inc(scanned, A_RING)
            first_rest(0)
            second_rest(0)
            for p in range(NPH):
                def pair(n, q, i):
                    for r in range(2):
                        u = NS * p + n + r
                        dve.wait_ge(b_ready, u + 1)
                        v.tensor_tensor(bank(2 * r, 2), du[:, p % 2, :], bank(2 * r, 2), ALU.mult).then_inc(u_done, 1)
                    for r in range(2):
                        u = NS * p + n + r
                        dve.wait_ge(u_done, u + 1)
                        dve.wait_ge(a_ready, u + 1)
                        dve.wait_ge(g_ready, u + 1)
                        v.tensor_tensor_scan(h_ring[:, r, :], a_ring[:, i + r, :], bank(2 * r, 2), 0.0,
                                             ALU.mult, ALU.add).then_inc(scanned, 1)

                dve.wait_ge(dt_ready, p + 1)
                pieces = {}
                if p > 0:
                    pieces[2] = lambda: normed(p - 1)
                    pieces[3] = lambda: residual(p - 1)
                if p + 1 < NPH:
                    pieces[5] = lambda: first_rest(p + 1)
                    pieces[6] = lambda: second_rest(p + 1)
                pairs_of(dve, pieces, pair)
            normed(NPH - 1)
            own.link(v.tensor_tensor(tok[:, :, :], tok[:, :, :], bdec_bc[:, None, :].broadcast_to([P, NT, D]), ALU.add))
            residual(NPH - 1)
            for g in range(NG):
                js = slice(TPG * g, TPG * (g + 1))
                dve.wait_ge(dec_psum, g + 1)
                own.link(v.tensor_tensor(tok[:, js, :], bank(g % 2).rearrange("p (q d) -> p q d", d=D), tok[:, js, :],
                                         ALU.add))
                v.memset(idf[:, 1, 0:1], 0.0).then_inc(tok_done, 1)
                moments(g).then_inc(var2_ready, 1)
                if g:
                    normalise(g - 1, rstd2_ready).then_inc(z2_ready, 1)
            normalise(NG - 1, rstd2_ready).then_inc(z2_ready, 1)
            bc_e = lambda x: x[:, None, :].broadcast_to([P, NT, NE])
            bc_t = lambda x: x[:, :, None].broadcast_to([P, NT, NE])
            logits = bank(4)[:, 0:NT * NE].rearrange("p (j e) -> p j e", e=NE)
            dve.wait_ge(logits_ready, 1)
            own.link(v.tensor_tensor(lg[:, :, :], logits, bc_e(br_bc), ALU.add))
            own.link(v.tensor_reduce(rmax[:, 0, :], lg[:, :, :], AX.X, ALU.max))
            v.tensor_tensor(lg[:, :, :], lg[:, :, :], bc_t(rmax[:, 0, :]), ALU.subtract).then_inc(shifted, 1)
            dve.wait_ge(exped, 1)
            own.link(v.tensor_reduce(rmax[:, 1, :], pr[:, :, :], AX.X, ALU.add))
            own.link(v.reciprocal(rmax[:, 2, :], rmax[:, 1, :]))
            own.link(v.tensor_tensor(pr[:, :, :], pr[:, :, :], bc_t(rmax[:, 2, :]), ALU.mult))
            for j in range(NT):
                n = own.mark(v.max(m8[:, j, :], pr[:, j, :]))
            own.need(n)
            for j in range(NT):
                n = own.mark(v.max_index(i8[:, j, :], m8[:, j, :], pr[:, j, :]))
            own.need(n)
            own.link(v.tensor_copy(i8f[:, :, :], i8[:, :, 0:TOPK]))
            for k in range(TOPK):
                n = own.mark(v.tensor_tensor(ohk[k][:, :, :], bc_e(iota_e), bc_t(i8f[:, :, k]), ALU.is_equal))
            own.need(n)
            v.tensor_tensor(routed[:, :, :], ohk[0][:, :, :], ohk[1][:, :, :], ALU.add).then_inc(counted, 1)
            own.link(v.tensor_tensor(rmax[:, 3, :], m8[:, :, 0], m8[:, :, 1], ALU.add))
            own.link(v.tensor_scalar(rmax[:, 3, :], rmax[:, 3, :], 1e-9, None, ALU.add))
            own.link(v.reciprocal(rmax[:, 0, :], rmax[:, 3, :]))
            for k in range(TOPK):
                own.link(v.tensor_tensor(wk[:, k, :], m8[:, :, k], rmax[:, 0, :], ALU.mult))
            dve.wait_ge(pos_ready, 1)
            by_e = lambda x: x.rearrange("p (j e) -> p e j", e=NE)
            own.link(v.tensor_copy(cnt[:, :, :], by_e(bank(6)[:, 0:NT * NE])))
            own.link(v.tensor_tensor_scan(cum[:, :, :].rearrange("p e j -> p (e j)"),
                                          not_first[:, :, :].rearrange("p e j -> p (e j)"),
                                          cnt[:, :, :].rearrange("p e j -> p (e j)"), 0.0, ALU.mult, ALU.add))
            own.link(v.tensor_tensor(cum[:, :, :], cum[:, :, :], cnt[:, :, :], ALU.subtract))
            own.link(v.tensor_tensor(pos[:, :, :], bank(5)[:, 0:NT * NE].rearrange("p (j e) -> p j e", e=NE),
                                     cum[:, :, :].rearrange("p e j -> p j e"), ALU.add))
            own.link(v.tensor_tensor(slot[:, :, :], pos[:, :, :], bc_e(iota_cap), ALU.add))
            for k in range(TOPK):
                for src, dst in ((pos, posk), (slot, slotk)):
                    own.link(v.tensor_tensor(tmp[:, :, :], ohk[k][:, :, :], src[:, :, :], ALU.mult))
                    own.link(v.tensor_reduce(dst[:, k, :], tmp[:, :, :], AX.X, ALU.add))
            own.link(v.tensor_scalar(keep[:, :, :], posk[:, :, :], float(CAP), None, ALU.is_lt))
            own.link(v.tensor_scalar(posk[:, :, :], keep[:, :, :], -float(2 * ROWS), float(2 * ROWS), ALU.mult, ALU.add))
            own.link(v.tensor_tensor(posk[:, :, :], posk[:, :, :], slotk[:, :, :], ALU.add))
            v.tensor_copy(into[:, :, :], posk[:, :, :]).then_inc(idx_made, 1)
            own.link(v.tensor_scalar(slotk[:, :, :], slotk[:, :, :], float(ROWS - 1), None, ALU.min))
            v.tensor_copy(outof[:, :, :], slotk[:, :, :]).then_inc(idx_made, 1)
            own.link(v.tensor_tensor(wk[:, :, :], wk[:, :, :], keep[:, :, :], ALU.mult))
            own.link(v.tensor_tensor(rmax[:, 0, :], wk[:, 0, :], wk[:, 1, :], ALU.add))
            own.link(v.tensor_scalar(rmax[:, 0, :], rmax[:, 0, :], 1e-9, None, ALU.add))
            own.link(v.reciprocal(rmax[:, 1, :], rmax[:, 0, :]))
            for k in range(TOPK):
                own.link(v.tensor_tensor(wk[:, k, :], wk[:, k, :], rmax[:, 1, :], ALU.mult))
            dve.sem_inc(out_copied, OUT_RING)
            dve.wait_ge(xeT_ready, 1)
            v.tensor_copy(xeT[0], bank(4, 2)[:, 0:CAP]).then_inc(xeT_copied, 1)

            def rows_next(e, i):
                dve.wait_ge(xeT_ready, e + 1)
                v.tensor_copy(xeT[i], bank(4, 2)[:, 0:CAP]).then_inc(xeT_copied, 1)

            def output(e, i):
                dve.wait_ge(out_psum, e + 1)
                dve.wait_ge(rows_out[i], 8 * (e - i) + 16)
                v.tensor_tensor(ob[i], bank(6, 2)[:, 0:CAP].rearrange("p (t d) -> p t d", d=D),
                                b2_bc[:, bass.ds(e, 1), :].broadcast_to([P, ST, D]), ALU.add).then_inc(out_copied, 1)

            with dve.Fori(0, NE // 2 - 1) as k:
                for i in range(2):
                    e = 2 * k
                    rows_next(e + i + 1, 1 - i)
                    output(e + i, i)
            rows_next(NE - 1, 1)
            for i in range(2):
                output(NE - 2 + i, i)
            for g in range(NG):
                dve.wait_ge(got[g], 16 * TOPK * TPG)
                for k in range(TOPK):
                    for j in range(TPG * g, TPG * (g + 1)):
                        ins = v.scalar_tensor_tensor(out_sb[:, j, :], picked[k][:, j, :], wk[:, k, j:j + 1],
                                                     (tok if k == 0 else out_sb)[:, j, :], ALU.mult, ALU.add)
                        if k == 0:
                            n = own.mark(ins)
                        else:
                            ins.then_inc(out_ready, 1)
                    own.need(n)

        @block.tensor
        def _(pe):
            v = nc.tensor

            def mm(out_ap, lhsT, rhs, start=True, stop=True):
                return v.matmul(out_ap, lhsT, rhs, start=start, stop=stop)

            def wide(out_ap, lhsT, rhs, start=True, stop=True):
                for o, r in zip(halves(out_ap), halves(rhs)):
                    last = mm(o, lhsT, r, start, stop)
                return last

            pe.wait_ge(consts_ready, 1)
            pe.wait_ge(weights_in, 16 * N_LOADS)
            mm(bank(0)[:, 0:NL], mean_w[:, :], cols[:, 2, :]).then_inc(bmix_mean, 1)
            pe.wait_ge(mean_ready, 1)
            for g in range(NG):
                pe.wait_ge(masked, g + 1)
                for q in range(TPG):
                    last = v.transpose(bank(0)[:, q * P:(q + 1) * P], xm[:, q, :], ident[:, :])
                last.then_inc(xT_ready, 1)
                if g > 0:
                    pe.wait_ge(hT_ready, g)
                if g % 2 == 0:
                    pe.wait_ge(oh_ready, g // 2 + 1)
                    js = slice(8 * (g // 2), 8 * (g // 2) + 8)
                    v.transpose(bank(7)[0:ET * 8, 0:P], oh[:, js, :].rearrange("p j e -> p (j e)"), ident[:, :])\
                        .then_inc(ohT_ready, 1)
                    pe.wait_ge(ohT_copied, g // 2 + 1)
                mm(bank(7), ohT[:, :], tokb_sel[:, TPG * (g % 2):TPG * (g % 2 + 1), :].rearrange("p j d -> p (j d)"))\
                    .then_inc(bias_ready, 1)
                pe.wait_ge(xT_copied, g + 1)
                for pr_ in range(2):
                    if g > 0:
                        pe.wait_ge(combined, 2 * (g - 1) + pr_ + 1)
                    b0 = 1 + 3 * pr_
                    for r in range(2):
                        x_ = xT[:, (2 * pr_ + r) * P:(2 * pr_ + r + 1) * P]
                        mm(bank(b0 + r), x_, tokw[:, 0:4, :].rearrange("p e d -> p (e d)"))
                        last = mm(bank(b0 + 2)[:, r * D:(r + 1) * D], x_, tokw[:, 4, :])
                    last.then_inc(y_tok_ready, 1)
                pe.wait_ge(z_ready, g + 1)
                pe.wait_ge(bias_copied, g + 1)
                for q in range(TPG):
                    last = v.transpose(bank(7)[:, q * P:(q + 1) * P], z[:, TPG * g + q, :], ident[:, :])
                last.then_inc(zT_ready, 1)

            def project_dt(p):
                if p >= NSEQ:
                    pe.wait_ge(h_next, p - NSEQ + 1)
                wide(W_PSUM, wdt[:, p // NSEQ, :], h_in(p)).then_inc(dt_psum, 1)

            def project_bc(p):
                pe.wait_ge(dt_parts, p + 1)
                wide(W_PSUM, wbc[:, p // NSEQ, :], h_in(p)).then_inc(bc_psum, 1)

            def spread_b(p, n, r):
                u = NS * p + n
                pe.wait_ge(scanned, u + 3)
                nn = n
                for h in range(2):
                    last = mm(bank(2 * r + h), sel[0:96, nn, :] if isinstance(nn, int) else
                              sel[0:96, bass.ds(nn, 1), :].rearrange("k a m -> k (a m)"),
                              split[p % 2][:, h * HALF:(h + 1) * HALF])
                last.then_inc(b_ready, 1)

            def add_y(p, n, r, stop=False):
                u = NS * p + n
                pe.wait_ge(g_ready, H_RING + u + 1)
                wide(Y_PSUM, ident[:, :], g_ring[:, r, :], False, stop).then_inc(y_added, 1)

            def mix(p):
                pe.wait_ge(gelu_done, p + 1)
                wide(W_PSUM, wmix[:, p // NSEQ, :], work[:, 0, :]).then_inc(mixed, 1)

            def variance(p):
                pe.wait_ge(squared, p + 1)
                wide(W_PSUM, mean_w[:, :], work[:, 0, :]).then_inc(var_psum, 1)

            pe.sem_inc(y_added, G_RING)
            pe.wait_ge(hT_ready, NG)
            pe.wait_ge(wbc_in, 16 * 8)
            project_dt(0)
            project_bc(0)
            pe.wait_ge(split_ready, 1)
            for r in range(2):
                spread_b(0, r, r)
            for p in range(NPH):
                if p > 0:
                    pe.wait_ge(gelu_done, p)
                wide(Y_PSUM, dskip[:, p // NSEQ, :], h_in(p), True, False)

                def pair(n, q, i):
                    for r in range(2):
                        spread_b(p, n + 2 + r, r)
                        add_y(p, n + r, r)

                pieces = {}
                if p > 0:
                    pieces[0] = lambda: mix(p - 1)
                    pieces[1] = lambda: variance(p - 1)
                if p + 1 < NPH:
                    pieces[3] = lambda: project_dt(p + 1)
                    pieces[4] = lambda: project_bc(p + 1)
                for q in range(NQ):
                    ks = (2 * q, 2 * q + 1)
                    if 2 * q in pieces or q == NQ - 1:
                        for k in ks:
                            if k == 2 * NQ - 1:
                                if p + 1 < NPH:
                                    pe.wait_ge(split_ready, p + 2)
                                for r in range(2):
                                    if p + 1 < NPH:
                                        spread_b(p + 1, r, r)
                                    add_y(p, 2 * k + r, r, stop=(r == 1))
                            else:
                                pair(2 * k, q, 0)
                            if k in pieces:
                                pieces[k]()
                    else:
                        with pe.Fori(0, GU // 2) as i:
                            pair(2 * i + GU * q, q, 2 * i)
                        if 2 * q + 1 in pieces:
                            pieces[2 * q + 1]()
                pe.wait_ge(y_added, G_RING + NS * (p + 1))
                pe.sem_inc(y_ready, 1)
            mix(NPH - 1)
            variance(NPH - 1)
            pe.wait_ge(h_next, NPH)
            for g in range(NG):
                if g >= 2:
                    pe.wait_ge(tok_done, g - 1)
                for q in range(TPG):
                    j = TPG * g + q
                    last = mm(bank(g % 2)[:, q * D:(q + 1) * D], hT[NL % 2][:, j * P:(j + 1) * P], wdec[:, :])
                last.then_inc(dec_psum, 1)
            for g in range(NG):
                pe.wait_ge(z2_ready, g + 1)
                if g >= 2:
                    pe.wait_ge(z2T_copied, g - 1)
                for q in range(TPG):
                    last = v.transpose(bank(2 + g % 2)[:, q * P:(q + 1) * P], z[:, TPG * g + q, :], ident[:, :])
                last.then_inc(z2T_ready, 1)
                pe.wait_ge(z2T_copied, g + 1)
                for q in range(TPG):
                    j = TPG * g + q
                    last = mm(bank(4)[:, j * NE:(j + 1) * NE], work[:, g % 2, q * P:(q + 1) * P], wr[:, :])
            last.then_inc(logits_ready, 1)
            pe.wait_ge(counted, 1)
            r_ = routed[:, :, :].rearrange("p j e -> p (j e)")
            mm(bank(5)[:, 0:NT * NE], tri[:, :], r_)
            mm(bank(6)[:, 0:NT * NE], ones_bf[:, :], r_).then_inc(pos_ready, 1)

            def rows_in_(e, i):
                pe.wait_ge(rows_in[i], 8 * (e - i) + 16)
                for t in range(ST):
                    last = v.transpose(bank(4, 2)[:, t * P:(t + 1) * P], xb[i][:, t, :], ident[:, :])
                last.then_inc(xeT_ready, 1)

            def hidden(e, i):
                pe.wait_ge(xeT_copied, e + 1)
                pe.wait_ge(w_in[i], 16 * (e - i) + 32)
                for f in range(FC):
                    pe.wait_ge(hid_ready, FC * e + f + 1)
                    for h in range(2):
                        last = mm(bank(2 * (f % 2) + h)[:, 0:CAP // 2], w1b[i][:, f * P:(f + 1) * P],
                                  xeT[i][:, h * CAP // 2:(h + 1) * CAP // 2])
                    last.then_inc(hid_psum, 1)

            def outputs(e, i):
                pe.wait_ge(hid_ready, FC * e + FC + HID_RING)
                pe.wait_ge(out_copied, e + 1)
                for t in range(ST):
                    for f in range(FC):
                        last = mm(bank(6, 2)[:, t * D:(t + 1) * D], hid[:, f, t * P:(t + 1) * P], w2b[i][:, f, :],
                                  f == 0, f == FC - 1)
                last.then_inc(out_psum, 1)

            rows_in_(0, 0)
            with pe.Fori(0, NE // 2 - 1) as k:
                for i in range(2):
                    e = 2 * k
                    hidden(e + i, i)
                    rows_in_(e + i + 1, 1 - i)
                    outputs(e + i, i)
            hidden(NE - 2, 0)
            rows_in_(NE - 1, 1)
            outputs(NE - 2, 0)
            hidden(NE - 1, 1)
            outputs(NE - 1, 1)


def kernel(x, L0_tok_emb_table, L0_tok_gate_table, L0_tok_expert_w, L0_tok_expert_b, L0_attn_A_log, L0_attn_W_B,
           L0_attn_b_B, L0_attn_W_C, L0_attn_b_C, L0_attn_W_dt, L0_attn_b_dt, L0_attn_D_skip, L0_attn_W_mix,
           L0_attn_b_mix, L0_attn_ln_g, L0_attn_ln_b, L0_attn_W_dec, L0_attn_b_dec, L0_ffn_Wr, L0_ffn_br,
           L0_ffn_W1, L0_ffn_b1, L0_ffn_W2, L0_ffn_b2):
    import numpy as np
    import concourse.bacc as bacc
    from concourse import mybir as my
    from concourse.bass_utils import run_bass_kernel_spmd

    n = lambda a: np.asarray(a)
    B, S = n(x).shape
    E, D, F = n(L0_ffn_W1).shape
    feature_first = lambda a: n(a).swapaxes(0, 1)
    arrays = {
        "ids": n(x).reshape(-1, 128).T, "emb_table": n(L0_tok_emb_table), "gate_table": n(L0_tok_gate_table),
        "tok_w": n(L0_tok_expert_w).transpose(2, 0, 1),
        "tok_b": np.tile(n(L0_tok_expert_b), (8, 1)),
        "A_log": feature_first(L0_attn_A_log), "W_B": feature_first(L0_attn_W_B), "b_B": n(L0_attn_b_B).T,
        "W_C": feature_first(L0_attn_W_C), "b_C": n(L0_attn_b_C).T, "W_dt": feature_first(L0_attn_W_dt),
        "b_dt": n(L0_attn_b_dt).T, "D_skip": n(L0_attn_D_skip).T, "W_mix": feature_first(L0_attn_W_mix),
        "b_mix": n(L0_attn_b_mix).T, "ln_g": n(L0_attn_ln_g).T, "ln_b": n(L0_attn_ln_b).T,
        "W_dec": n(L0_attn_W_dec), "b_dec": n(L0_attn_b_dec)[None, :], "Wr": n(L0_ffn_Wr),
        "br": n(L0_ffn_br)[None, :], "W1": n(L0_ffn_W1).transpose(1, 0, 2),
        "b1": n(L0_ffn_b1).reshape(E, F // 128, 128).transpose(2, 0, 1),
        "W2": n(L0_ffn_W2).reshape(E, F // 128, 128, D).transpose(2, 0, 1, 3).reshape(128, E, F // 128 * D),
        "b2": n(L0_ffn_b2)[None, :, :],
    }
    arrays = {k: np.ascontiguousarray(a) for k, a in arrays.items()}
    nc = bacc.Bacc("TRN2", target_bir_lowering=False, num_devices=1)
    args = [nc.dram_tensor("in_" + k, a.shape, my.dt.from_np(a.dtype), kind="ExternalInput").ap()
            for k, a in arrays.items()]
    out = nc.dram_tensor("out", [128, B * S // 128, D], my.dt.float32, kind="ExternalOutput").ap()
    tower_kernel(nc, *args, out)
    r = run_bass_kernel_spmd(nc, [{"in_" + k: a for k, a in arrays.items()}], core_ids=[0])
    got = r.results[0]["out"]
    return got.transpose(1, 0, 2).reshape(B, S, D)
```

```python
import concourse.bass as bass
from concourse import mybir
from contextlib import ExitStack

F32, BF16 = mybir.dt.float32, mybir.dt.bfloat16
I32, U32 = mybir.dt.int32, mybir.dt.uint32
ALU = mybir.AluOpType
ACT = mybir.ActivationFunctionType
AX = mybir.AxisListType


class Chain:

    def __init__(self, engine, semaphore):
        self.engine, self.semaphore, self.count = engine, semaphore, 0

    def mark(self, instruction):
        instruction.then_inc(self.semaphore, 1)
        self.count += 1
        return self.count

    def need(self, count):
        self.engine.wait_ge(self.semaphore, count)

    def link(self, instruction):
        self.need(self.mark(instruction))


def tower_kernel(nc, ids, emb_gate, tok_w, tok_b, A_log, W_B, b_B, W_C, b_C, W_dt, b_dt,
                 D_skip, W_mix, b_mix, ln_g, ln_b, W_dec, b_dec, Wr, br, W1, b1, W2, b2, out):
    P = 128
    VOCAB, D = emb_gate.shape[0], emb_gate.shape[1] - 1
    NT = ids.shape[1]
    T = NT * P
    NSEQ, L = 2, T // 2
    NL = A_log.shape[1]
    NS = A_log.shape[2]
    ET = tok_w.shape[1]
    NE = Wr.shape[1]
    FF = W1.shape[2]
    FC = FF // P
    TOPK = 2
    CAP = -(-5 * T * TOPK // (4 * NE))
    ROWS = NE * CAP
    ST = CAP // P
    HALF = 512
    TPG = HALF // D
    NG = NT // TPG
    NPH = NL * NSEQ
    GU = 4
    NQ = NS // GU
    EPS = 1e-5
    STEP = D // ET
    EXACT = float(2 ** 23)
    N_LOADS = 14
    assert ROWS % P == 0 and CAP % P == 0 and NS == 16

    x_rows = nc.dram_tensor("x_rows", [ROWS, D], F32, kind="Internal").ap()
    y_rows = nc.dram_tensor("y_rows", [ROWS, D], F32, kind="Internal").ap()
    c_dram = nc.dram_tensor("c_dram", [NPH, NS, L], F32, kind="Internal").ap()

    ctx = ExitStack()
    with ctx:
        def sb(name, shape, dt=F32):
            return ctx.enter_context(nc.sbuf_tensor(name, shape, dt))

        def sem(name):
            return ctx.enter_context(nc.semaphore(name))

        ident = sb("ident", [P, P])
        iota_d = sb("iota_d", [P, P])
        sel = sb("sel", [P, NS, P], BF16)
        tri = sb("tri", [P, P], BF16)
        ones_bf = sb("ones_bf", [P, P], BF16)
        mean_w = sb("mean_w", [P, P])
        iota_e = sb("iota_e", [P, NE])
        iota_cap = sb("iota_cap", [P, NE])
        not_first = sb("not_first", [P, NE, NT])
        eps_col = sb("eps_col", [P, 1])
        one_col = sb("one_col", [P, 1])
        tokw = sb("tokw", [P, ET, D])
        negA = sb("negA", [P, NL, NS])
        wbc = sb("wbc", [P, NL, P])
        bbc = sb("bbc", [P, NL])
        wdt = sb("wdt", [P, NL, D])
        wmix = sb("wmix", [P, NL, D])
        cols = sb("cols", [P, 5, NL])
        dskip = sb("dskip", [P, NL, D])
        wdec = sb("wdec", [P, D])
        bdec_bc = sb("bdec_bc", [P, D])
        wr = sb("wr", [P, NE])
        br_bc = sb("br_bc", [P, NE])
        b1_sb = sb("b1_sb", [P, NE, FC])
        b2_bc = sb("b2_bc", [P, NE, D])
        ids_sb = sb("ids_sb", [P, NT], I32)
        idf = sb("idf", [P, 2, NT])
        idx = sb("idx", [P, NT], U32)
        gate = sb("gate", [P, 5, NT])
        gate_i = sb("gate_i", [P, NT], I32)
        ge = sb("ge", [P, NT, ET - 1])
        oh = sb("oh", [P, NT, ET])
        tok = sb("tok", [P, NT, D])
        stats = sb("stats", [P, NT, 6])
        mv = sb("mv", [P, NT, 2])
        rstd = sb("rstd", [P, 3, NT])
        hT = [sb(f"hT{i}", [P, T]) for i in range(2)]
        dt = sb("dt", [P, 2, L])
        du = sb("du", [P, 2, L])
        bc = sb("bc", [P, L])
        rest = sb("rest", [96, L])
        part = sb("part", [96, L], BF16)
        split = [sb(f"split{i}", [96, L], BF16) for i in range(2)]
        a_ring = sb("a_ring", [P, GU, L])
        h_ring = sb("h_ring", [P, GU, L])
        g_ring = sb("g_ring", [P, GU, L])
        work = sb("work", [P, 2, L])
        big = sb("big", [P, NS, L])
        z = h_ring[:, 2:4, :].rearrange("p a b -> p (a b)").rearrange("p (j d) -> p j d", d=D)
        out_sb = h_ring[:, 0:2, :].rearrange("p a b -> p (a b)").rearrange("p (j d) -> p j d", d=D)

        ps = ctx.enter_context(nc.psum_tensor("ps", [P, 8 * HALF], F32))

        def bank(i, n=1):
            return ps[:, i * HALF:(i + n) * HALF]

        emb = big[:, 0:3, :].rearrange("p a b -> p (a b)")[:, 0:NT * (D + 1)].rearrange("p (j d) -> p j d", d=D + 1)
        mk = big[:, 14, 0:HALF].rearrange("p (q d) -> p q d", d=D)
        xm = [big[:, 3, i * HALF:(i + 1) * HALF].rearrange("p (q d) -> p q d", d=D) for i in range(2)]
        xT = [big[:, 15, i * HALF:(i + 1) * HALF] for i in range(2)]
        zero = big[:, 4:14, :].rearrange("p a b -> p (a b)")[:, 0:ROWS * D // P]
        flat = big[:, :, :].rearrange("p a b -> p (a b)")
        w1b = [flat[:, i * FF:(i + 1) * FF] for i in range(2)]
        w2b = [flat[:, (2 + i) * FF:(3 + i) * FF].rearrange("p (c d) -> p c d", d=D) for i in range(2)]
        o0 = 4 * FF
        xb = [flat[:, o0 + i * CAP:o0 + (i + 1) * CAP].rearrange("p (t d) -> p t d", d=D) for i in range(2)]
        xeT = [flat[:, o0 + (2 + i) * CAP:o0 + (3 + i) * CAP] for i in range(2)]
        ob = [flat[:, o0 + (4 + i) * CAP:o0 + (5 + i) * CAP].rearrange("p (t d) -> p t d", d=D) for i in range(2)]
        o1 = o0 + 6 * CAP
        hid = flat[:, o1:o1 + FC * CAP].rearrange("p (f c) -> p f c", f=FC)
        picked = [a_ring[:, 2 * k:2 * k + 2, :].rearrange("p a b -> p (a b)").rearrange("p (j d) -> p j d", d=D)
                  for k in range(TOPK)]
        lg = sb("lg", [P, NT, NE])
        pr = sb("pr", [P, NT, NE])
        rmax = sb("rmax", [P, 4, NT])
        m8 = sb("m8", [P, NT, 8])
        i8 = sb("i8", [P, NT, 8], U32)
        i8f = sb("i8f", [P, NT, TOPK])
        ohk = [sb(f"ohk{k}", [P, NT, NE]) for k in range(TOPK)]
        routed = sb("routed", [P, NT, NE], BF16)
        cnt = sb("cnt", [P, NE, NT])
        cum = sb("cum", [P, NE, NT])
        pos = sb("pos", [P, NT, NE])
        slot = sb("slot", [P, NT, NE])
        tmp = sb("tmp", [P, NT, NE])
        wk = sb("wk", [P, TOPK, NT])
        posk = sb("posk", [P, TOPK, NT])
        keep = sb("keep", [P, TOPK, NT])
        slotk = sb("slotk", [P, TOPK, NT])
        into = sb("into", [P, TOPK, NT], U32)
        outof = sb("outof", [P, TOPK, NT], U32)

        (ids_in, tok_in, weights_in, wbc_in, wbc_zero, idx_ready, consts_ready, zero_ready, zeroed, negA_ready,
         filled, ident_ready, sel_ready, biases_zero, shift_ready,
         mean_ready, bmix_mean, folded, masked, xT_ready, xT_copied, biases_in, biases_ready,
         y_tok_ready, combined, var_ready, rstd_ready, z_ready, zT_ready, hT_ready,
         dt_psum, dt_parts, dt_ready, bc_psum, bc_ready, c_stored, split_first, split_second, split_ready,
         b_ready, a_ready, u_done, scanned, g_ready, y_added, y_ready, gelu_done, mixed, squared, centred, var_psum,
         rstd_psum, z_psum, z_scaled, h_next, bdec_added, dec_psum, tok_done, var2_ready, rstd2_ready, z2_ready,
         z2T_ready, z2T_copied, logits_ready, shifted, exped, counted, pos_ready, idx_made, scattered,
         xeT_ready, xeT_copied, hid_psum, hid_ready, out_psum, out_copied, out_ready, out_stored,
         chain_dve, chain_pool, chain_act) = [sem(name) for name in """
            ids_in tok_in weights_in wbc_in wbc_zero idx_ready consts_ready zero_ready zeroed negA_ready
            filled ident_ready sel_ready biases_zero shift_ready
            mean_ready bmix_mean folded masked xT_ready xT_copied biases_in biases_ready
            y_tok_ready combined var_ready rstd_ready z_ready zT_ready hT_ready
            dt_psum dt_parts dt_ready bc_psum bc_ready c_stored split_first split_second split_ready
            b_ready a_ready u_done scanned g_ready y_added y_ready gelu_done mixed squared centred var_psum
            rstd_psum z_psum z_scaled h_next bdec_added dec_psum tok_done var2_ready rstd2_ready z2_ready
            z2T_ready z2T_copied logits_ready shifted exped counted pos_ready idx_made scattered
            xeT_ready xeT_copied hid_psum hid_ready out_psum out_copied out_ready out_stored
            chain_dve chain_pool chain_act""".split()]
        emb_in = [sem(f"emb_in{i}") for i in range(NSEQ)]
        c_in = [sem(f"c_in{q}") for q in range(NQ)]
        w_in = [sem(f"w_in{i}") for i in range(2)]
        rows_in = [sem(f"rows_in{i}") for i in range(2)]
        rows_out = [sem(f"rows_out{i}") for i in range(2)]
        got = [sem(f"got{g}") for g in range(NG)]
        block = ctx.enter_context(nc.Block())

        def halves(ap):
            return [ap[:, h * HALF:(h + 1) * HALF] for h in range(2)]


        def tokens(p):
            return slice((p % NSEQ) * L, (p % NSEQ + 1) * L)

        def h_in(p):
            return hT[p // NSEQ % 2][:, tokens(p)]

        def h_out(p):
            return hT[(p // NSEQ + 1) % 2][:, tokens(p)]

        def dt_banks(p):
            return two_banks(p if p else 1)

        def units_of(engine, pieces, pair):
            def behind(n):
                for piece in pieces.get(n, []) if isinstance(n, int) else []:
                    piece()

            for q in range(NQ):
                n0 = GU * q
                if any(n in pieces for n in range(n0, n0 + GU - 1)):
                    for i in range(0, GU, 2):
                        pair(n0 + i, q, i, behind)
                        behind(n0 + i + 1)
                else:
                    with engine.Fori(0, GU // 2) as k:
                        pair(2 * k + n0, q, 2 * k, behind)
                    behind(n0 + GU - 1)

        H_RING, A_RING, G_RING = GU, GU, GU
        HID_RING, OUT_RING = 2, 1
        Y_LAG = 1
        PE_POST = (3, 4)
        PE_PREP = (8, 11)
        ACT_POST = (3, 5, 7, 11)
        ACT_PREP = (11, 14, 15)
        DVE_POST = (6, 8)
        DVE_PREP = (11, 14)
        POOL_DT = 13

        def two_banks(p):
            return bank(4 + 2 * (p % 2), 2)

        @block.sync
        def _(sp):
            sp.dma_start(ids_sb[:, :], ids).then_inc(ids_in, 16)
            sp.dma_start(tokw[:, :, :], tok_w).then_inc(tok_in, 16)
            sp.wait_ge(biases_zero, 1)
            for i in range(3):
                sp.dma_start(bc[32 * i:32 * i + 1, 0:ET * D], tok_b).then_inc(biases_in, 16)
            loads = [(wmix[:, :, :], W_mix), (negA[:, :, :], A_log), (wdt[:, :, :], W_dt),
                     (wdec[:, :], W_dec), (wr[:, :], Wr), (b1_sb[:, :, :], b1),
                     (bdec_bc[:, :], b_dec.broadcast_to([P, D])), (br_bc[:, :], br.broadcast_to([P, NE])),
                     (b2_bc[:, :, :], b2.broadcast_to([P, NE, D]))]
            loads += [(cols[:, i, :], c) for i, c in enumerate((b_dt, D_skip, b_mix, ln_g, ln_b))]
            assert len(loads) == N_LOADS
            for dst, src in loads:
                sp.dma_start(dst, src).then_inc(weights_in, 16)
            sp.wait_ge(wbc_zero, 2)
            for i, (w, b) in enumerate(((W_B, b_B), (W_B, b_B), (W_B, b_B), (W_C, b_C))):
                sp.dma_start(wbc[:, :, 32 * i:32 * i + NS], w).then_inc(wbc_in, 16)
                sp.dma_start(bbc[32 * i:32 * i + NS, :], b).then_inc(wbc_in, 16)
            sp.wait_ge(zero_ready, 1)
            sp.wait_ge(emb_in[1], 16 * NT // NSEQ)
            sp.dma_start(x_rows.rearrange("(p n) d -> p (n d)", p=P), zero).then_inc(zeroed, 16)
            for p in range(NPH):
                sp.wait_ge(bc_ready, 2 * (p + 1))
                sp.dma_start(c_dram[p, :, :], bc[96:96 + NS, :]).then_inc(c_stored, 16)
                sp.wait_ge(c_stored, 16 * (p + 1))
                if p == 0:
                    sp.wait_ge(hT_ready, NG)
                    sp.wait_ge(zeroed, 16)
                for q in range(NQ):
                    if p > 0:
                        sp.wait_ge(g_ready, H_RING + NS * (p - 1) + GU * (q + 1))
                    sp.dma_start(big[:, GU * q:GU * (q + 1), :],
                                 c_dram[p:p + 1, GU * q:GU * (q + 1), :].broadcast_to([P, GU, L]))\
                        .then_inc(c_in[q], 16)

            w1_v = W1.rearrange("d e f -> d e f")
            rows_v = x_rows.rearrange("(e t p) d -> p e t d", p=P, e=NE)
            out_v = y_rows.rearrange("(e t p) d -> p e t d", p=P, e=NE)

            def load_weights(e, i):
                sp.dma_start(w1b[i], w1_v[:, e, :]).then_inc(w_in[i], 16)
                sp.dma_start(w2b[i].rearrange("p c d -> p (c d)"), W2[:, e, :]).then_inc(w_in[i], 16)

            def load_rows(e, i):
                sp.dma_start(xb[i], rows_v[:, e, :, :]).then_inc(rows_in[i], 16)

            def store_rows(e, i):
                sp.wait_ge(out_copied, OUT_RING + e + 1)
                sp.dma_start(out_v[:, e, :, :], ob[i]).then_inc(rows_out[i], 16)

            sp.wait_ge(g_ready, H_RING + NS * NPH)
            for i in range(2):
                sp.sem_inc(rows_out[i], 16)
                load_weights(i, i)
            sp.wait_ge(scattered, 16 * TOPK * NT)
            for i in range(2):
                load_rows(i, i)
            with sp.Fori(0, NE // 2 - 1) as k:
                for i in range(2):
                    e = 2 * k
                    sp.wait_ge(out_psum, e + i + 1)
                    load_weights(e + i + 2, i)
                    load_rows(e + i + 2, i)
                    store_rows(e + i, i)
            for i in range(2):
                store_rows(NE - 2 + i, i)
            for h in range(NSEQ):
                sp.wait_ge(out_ready, NT // NSEQ * (h + 1))
                js = slice(h * NT // NSEQ, (h + 1) * NT // NSEQ)
                sp.dma_start(out[:, js, :], out_sb[:, js, :]).then_inc(out_stored, 16)
            sp.wait_ge(out_stored, 16 * NSEQ)

        @block.gpsimd
        def _(pool):
            v = nc.gpsimd
            own = Chain(pool, chain_pool)
            v.iota(iota_d[:, :], [[1, P]], 0, 0, allow_small_or_imprecise_dtypes=True)
            own.link(v.memset(ident[:, :], 0.0))
            v.affine_select(ident[:, :], ident[:, :], [[-1, P]], ALU.not_equal, 1.0, 0, 1).then_inc(ident_ready, 1)

            def gather(h):
                for j in range(h * NT // NSEQ, (h + 1) * NT // NSEQ):
                    v.indirect_dma_start(emb[:, j, :], None, emb_gate,
                                         bass.IndirectOffsetOnAxis(ap=idx[:, j:j + 1], axis=0)).then_inc(emb_in[h], 16)

            def select_rows(k):
                return v.affine_select(sel[:, :, :], sel[:, :, :], [[-1, NS], [0, P]], ALU.not_equal, 1.0, -32 * k, 1)

            pool.wait_ge(idx_ready, 1)
            gather(0)
            pool.wait_ge(filled, 1)
            own.link(select_rows(0))
            own.link(select_rows(1))
            select_rows(2).then_inc(sel_ready, 1)
            gather(1)
            v.affine_select(tri[:, :], ones_bf[:, :], [[1, P]], ALU.is_gt, 0.0, 0, -1)
            v.iota(iota_e[:, :], [[1, NE]], 0, 0, allow_small_or_imprecise_dtypes=True)
            v.iota(iota_cap[:, :], [[CAP, NE]], 0, 0, allow_small_or_imprecise_dtypes=True).then_inc(consts_ready, 1)

            def step_size(p):
                pool.wait_ge(dt_parts, p + 1)
                own.link(v.tensor_tensor(dt[:, p % 2, :], work[:, 0, :], work[:, 1, :], ALU.add))
                v.tensor_tensor(du[:, p % 2, :], dt[:, p % 2, :], h_in(p), ALU.mult).then_inc(dt_ready, 1)

            pool.sem_inc(g_ready, H_RING)
            for p in range(NPH):
                def pair(n, q, i, behind):
                    pool.wait_ge(c_in[q], 16 * (p + 1))
                    for r in range(2):
                        u = NS * p + n + r
                        pool.wait_ge(scanned, A_RING + u + 1)
                        pool.wait_ge(y_added, u + 1)
                        v.tensor_tensor(g_ring[:, i + r, :], h_ring[:, i + r, :], big[:, n + r, :], ALU.mult)\
                            .then_inc(g_ready, 1)
                        if r == 0:
                            behind(n)

                units_of(pool, {POOL_DT: [lambda: step_size(p + 1)]} if p + 1 < NPH else {}, pair)
            pool.wait_ge(zeroed, 16)
            pool.wait_ge(idx_made, 2)
            for k in range(TOPK):
                for j in range(NT):
                    v.indirect_dma_start(x_rows, bass.IndirectOffsetOnAxis(ap=into[:, k, j:j + 1], axis=0),
                                         z[:, j, :], None, bounds_check=ROWS - 1, oob_is_err=False)\
                        .then_inc(scattered, 16)
            for i in range(2):
                pool.wait_ge(rows_out[i], 16 + 16 * NE // 2)
            for j in range(NT):
                for k in range(TOPK):
                    v.indirect_dma_start(picked[k][:, j, :], None, y_rows,
                                         bass.IndirectOffsetOnAxis(ap=outof[:, k, j:j + 1], axis=0))\
                        .then_inc(got[j // TPG], 16)

        @block.scalar
        def _(act):
            v = nc.scalar
            own = Chain(act, chain_act)
            v.preload_act_table_set("natural_log_exp_and_others")
            act.wait_ge(weights_in, 16 * N_LOADS)
            own.link(v.activation(negA[:, :, :], negA[:, :, :], ACT.Exp))
            v.activation(negA[:, :, :], negA[:, :, :], ACT.Copy, scale=-1.0).then_inc(negA_ready, 1)

            def reciprocal_root(dst, var, tmp):
                own.link(v.activation(tmp, var, ACT.Ln, bias=eps_col[:, :]))
                return v.activation(dst, tmp, ACT.Exp, scale=-0.5)

            def copy_xT(g):
                act.wait_ge(xT_ready, g + 1)
                if g >= 2:
                    act.wait_ge(y_tok_ready, 2 * (g - 1))
                v.activation(xT[g % 2], bank(0), ACT.Copy).then_inc(xT_copied, 1)

            def normalise(g):
                js = slice(TPG * g, TPG * (g + 1))
                act.wait_ge(var_ready, g + 1)
                reciprocal_root(rstd[:, 0, js], mv[:, js, 1], rstd[:, 1, js]).then_inc(rstd_ready, 1)
                act.wait_ge(shift_ready, g + 1)
                for j in range(TPG * g, TPG * (g + 1)):
                    last = v.activation(z[:, j, :], tok[:, j, :], ACT.Identity, bias=rstd[:, 2, j:j + 1],
                                        scale=rstd[:, 0, j:j + 1])
                last.then_inc(z_ready, 1)

            def copy_hT(g):
                act.wait_ge(zT_ready, g + 1)
                v.activation(hT[0][:, HALF * g:HALF * (g + 1)], bank(7), ACT.Copy).then_inc(hT_ready, 1)

            copy_xT(0)
            for g in range(NG):
                if g > 0:
                    normalise(g - 1)
                if g + 1 < NG:
                    copy_xT(g + 1)
                if g > 0:
                    copy_hT(g - 1)
            normalise(NG - 1)
            copy_hT(NG - 1)

            def softplus_parts(p):
                l = p // NSEQ
                act.wait_ge(dt_psum, p + 1)
                own.link(v.activation(work[:, 0, :], dt_banks(p), ACT.Abs, bias=cols[:, 0, l:l + 1]))
                v.activation(work[:, 1, :], dt_banks(p), ACT.Relu, bias=cols[:, 0, l:l + 1]).then_inc(chain_act, 1)
                own.count += 1
                own.link(v.activation(work[:, 0, :], work[:, 0, :], ACT.Exp, scale=-1.0))
                v.activation(work[:, 0, :], work[:, 0, :], ACT.Ln, bias=one_col[:, :]).then_inc(dt_parts, 1)

            def b_and_c(p):
                l = p // NSEQ
                act.wait_ge(bc_psum, p + 1)
                if p > 0:
                    act.wait_ge(c_stored, 16 * p)
                    act.wait_ge(split_ready, p)
                v.activation(bc[:, :], two_banks(p), ACT.Identity, bias=bbc[:, l:l + 1]).then_inc(bc_ready, 1)
                v.activation(split[p % 2][:, :], two_banks(p)[0:96, :], ACT.Identity, bias=bbc[0:96, l:l + 1])\
                    .then_inc(bc_ready, 1)

            def second_part(p):
                act.wait_ge(split_first, p + 1)
                v.activation(part[:, :], rest[:, :], ACT.Copy).then_inc(split_second, 1)

            def gelu(p):
                act.wait_ge(y_ready, p + 1)
                v.activation(work[:, 0, :], two_banks(p), ACT.Gelu).then_inc(gelu_done, 1)
                v.preload_act_table_set("natural_log_exp_and_others")

            def centre(p):
                l = p // NSEQ
                act.wait_ge(mixed, p + 1)
                v.activation(work[:, 0, :], two_banks(p), ACT.Square, bias=cols[:, 2, l:l + 1]).then_inc(squared, 1)
                v.activation(work[:, 1, :], two_banks(p), ACT.Identity, bias=cols[:, 2, l:l + 1]).then_inc(centred, 1)

            def root(p):
                act.wait_ge(var_psum, p + 1)
                reciprocal_root(two_banks(p), two_banks(p), two_banks(p)).then_inc(rstd_psum, 1)

            def scale_norm(p):
                l = p // NSEQ
                act.wait_ge(z_psum, p + 1)
                v.activation(two_banks(p), two_banks(p), ACT.Identity, bias=cols[:, 4, l:l + 1], scale=cols[:, 3, l:l + 1])\
                    .then_inc(z_scaled, 1)

            b_and_c(0)
            second_part(0)
            softplus_parts(0)
            for p in range(NPH):
                def pair(n, q, i, behind):
                    for r in range(2):
                        u = NS * p + n + r
                        act.wait_ge(scanned, u + 1)
                        nn = n + r
                        v.activation(a_ring[:, i + r, :], dt[:, p % 2, :], ACT.Exp,
                                     scale=negA[:, p // NSEQ, bass.ds(nn, 1)]).then_inc(a_ready, 1)
                        if r == 0:
                            behind(n)

                act.wait_ge(dt_ready, p + 1)
                pieces = {}
                if p > 0:
                    for n, piece in zip(ACT_POST, (gelu, centre, root, scale_norm)):
                        pieces.setdefault(n, []).append(lambda piece=piece: piece(p - 1))
                if p + 1 < NPH:
                    for n, piece in zip(ACT_PREP, (b_and_c, second_part, softplus_parts)):
                        pieces.setdefault(n, []).append(lambda piece=piece: piece(p + 1))
                units_of(act, pieces, pair)
            last = NPH - 1
            gelu(last)
            centre(last)
            root(last)
            scale_norm(last)
            for g in range(NG):
                js = slice(TPG * g, TPG * (g + 1))
                act.wait_ge(var2_ready, g + 1)
                reciprocal_root(rstd[:, 0, js], mv[:, js, 1], rstd[:, 1, js]).then_inc(rstd2_ready, 1)
                act.wait_ge(z2T_ready, g + 1)
                v.activation(work[:, g % 2, 0:HALF], bank(2 + g % 2), ACT.Copy).then_inc(z2T_copied, 1)
            act.wait_ge(shifted, 1)
            v.activation(pr[:, :, :], lg[:, :, :], ACT.Exp).then_inc(exped, 1)
            act.sem_inc(hid_ready, HID_RING)
            v.preload_act_table_set("gelu_and_others")
            with act.Fori(0, NE) as e:
                for f in range(FC):
                    act.wait_ge(hid_psum, FC * e + f + 1)
                    v.activation(hid[:, f, :].rearrange("p (a b) -> p a b", a=2),
                                 bank(2 * (f % 2), 2).rearrange("p (a b) -> p a b", a=2)[:, :, 0:CAP // 2],
                                 ACT.Gelu, bias=b1_sb[:, e, f:f + 1]).then_inc(hid_ready, 1)

        @block.vector
        def _(dve):
            v = nc.vector
            own = Chain(dve, chain_dve)
            v.memset(eps_col[:, :], EPS)
            v.memset(one_col[:, :], 1.0)
            dve.wait_ge(ids_in, 16)
            own.link(v.tensor_copy(idf[:, 0, :], ids_sb[:, :]))
            own.link(v.tensor_scalar(idf[:, 1, :], idf[:, 0, :], 0.0, float(VOCAB), ALU.is_lt, ALU.mult))
            own.link(v.tensor_tensor(idf[:, 0, :], idf[:, 0, :], idf[:, 1, :], ALU.add))
            own.link(v.tensor_scalar(idf[:, 0, :], idf[:, 0, :], 0.0, float(VOCAB - 1), ALU.max, ALU.min))
            v.tensor_copy(idx[:, :], idf[:, 0, :]).then_inc(idx_ready, 1)
            v.memset(bc[0:96, 0:ET * D], 0.0).then_inc(biases_zero, 1)
            v.memset(wbc[:, :, :], 0.0).then_inc(wbc_zero, 1)
            v.memset(bbc[:, :], 0.0).then_inc(wbc_zero, 1)
            v.memset(mean_w[:, :], 1.0 / D)
            v.memset(not_first[:, :, :], 1.0)
            v.memset(ones_bf[:, :], 1.0)
            own.link(v.memset(sel[:, :, :], 0.0))
            v.memset(not_first[:, :, 0:1], 0.0).then_inc(filled, 1)
            v.memset(zero, 0.0).then_inc(zero_ready, 1)
            bias, first, left, second = bc[0:96, 0:ET * D], split[1][:, 0:ET * D], rest[:, 0:ET * D], part[:, 0:ET * D]
            dve.wait_ge(biases_in, 16 * 3)
            own.link(v.tensor_copy(first, bias))
            own.link(v.tensor_tensor(left, bias, first, ALU.subtract))
            own.link(v.tensor_copy(second, left))
            own.link(v.tensor_tensor(left, left, second, ALU.subtract))
            v.tensor_copy(first[32:64, :], second[32:64, :])
            v.tensor_copy(first[64:96, :], left[64:96, :]).then_inc(biases_ready, 1)
            dve.wait_ge(weights_in, 16 * N_LOADS)
            dve.wait_ge(ident_ready, 1)
            own.link(v.tensor_reduce(idf[:, 0, 0:NL], wmix[:, :, :], AX.X, ALU.add))
            own.link(v.tensor_scalar(idf[:, 0, 0:NL], idf[:, 0, 0:NL], 1.0 / D, None, ALU.mult))
            for l in range(NL):
                own.link(v.tensor_scalar(wmix[:, l, :], wmix[:, l, :], idf[:, 0, l:l + 1], None, ALU.subtract))
                own.link(v.tensor_scalar(dskip[:, l, :], ident[:, :], cols[:, 1, l:l + 1], None, ALU.mult))
            dve.wait_ge(bmix_mean, 1)
            v.tensor_tensor(cols[:, 2, :], cols[:, 2, :], bank(0)[:, 0:NL], ALU.subtract).then_inc(mean_ready, 1)

            def gates(h):
                js = slice(h * NT // NSEQ, (h + 1) * NT // NSEQ)
                n = NT // NSEQ
                g, c, fl, ab, fr = [gate[:, i, js] for i in range(5)]
                raw = emb[:, js, D]
                dve.wait_ge(emb_in[h], 16 * n)
                own.link(v.tensor_scalar(g, raw, float(D), None, ALU.mult))
                own.link(v.tensor_scalar(c, g, 1e9, None, ALU.mult))
                own.link(v.tensor_scalar(c, c, -EXACT, EXACT, ALU.max, ALU.min))
                own.link(v.tensor_copy(gate_i[:, js], c))
                own.link(v.tensor_copy(fl, gate_i[:, js]))
                own.link(v.tensor_tensor(ab, fl, c, ALU.is_gt))
                own.link(v.tensor_tensor(fl, fl, ab, ALU.subtract))
                own.link(v.tensor_tensor(fr, c, fl, ALU.subtract))
                own.link(v.tensor_scalar(fr, fr, 1e-9, None, ALU.mult))
                for k in range(1, ET):
                    own.link(v.tensor_scalar(ge[:, js, k - 1], g, float(k * STEP - 1), None, ALU.is_gt))
                own.link(v.tensor_scalar(oh[:, js, 0], ge[:, js, 0], -1.0, 1.0, ALU.mult, ALU.add))
                for k in range(1, ET - 1):
                    own.link(v.tensor_tensor(oh[:, js, k], ge[:, js, k - 1], ge[:, js, k], ALU.subtract))
                own.link(v.tensor_copy(oh[:, js, ET - 1], ge[:, js, ET - 2]))

            def mask(g):
                if g > 0:
                    dve.wait_ge(masked, g)
                if g >= 2:
                    dve.wait_ge(xT_ready, g - 1)
                for q in range(TPG):
                    j = TPG * g + q
                    n = own.mark(v.tensor_scalar(mk[:, q, :], iota_d[:, :], gate[:, 0, j:j + 1],
                                                 gate[:, 4, j:j + 1], ALU.is_lt, ALU.add))
                own.need(n)
                for q in range(TPG):
                    last = v.tensor_tensor(xm[g % 2][:, q, :], emb[:, TPG * g + q, 0:D], mk[:, q, :], ALU.mult)
                last.then_inc(masked, 1)

            def normalise(g, ready):
                dve.wait_ge(ready, g + 1)
                for j in range(TPG * g, TPG * (g + 1)):
                    last = v.tensor_scalar(z[:, j, :], tok[:, j, :], mv[:, j, 0:1], rstd[:, 0, j:j + 1],
                                           ALU.subtract, ALU.mult)
                return last

            def moments(g):
                for j in range(TPG * g, TPG * (g + 1)):
                    n = own.mark(v.bn_stats(stats[:, j, :], tok[:, j, :]))
                own.need(n)
                for j in range(TPG * g, TPG * (g + 1)):
                    last = v.bn_aggr(mv[:, j, :], stats[:, j, :])
                return last

            def combine(g, pr_):
                dve.wait_ge(y_tok_ready, 2 * g + pr_ + 1)
                b0 = 1 + 3 * pr_
                done = [0, 0]
                for e in range(ET):
                    for r in range(2):
                        j = TPG * g + 2 * pr_ + r
                        y = bank(b0 + r)[:, e * D:(e + 1) * D] if e < 4 else bank(b0 + 2)[:, r * D:(r + 1) * D]
                        if e:
                            own.need(done[r])
                        if e == 0:
                            ins = v.tensor_scalar(tok[:, j, :], y, oh[:, j, 0:1], None, ALU.mult)
                        else:
                            ins = v.scalar_tensor_tensor(tok[:, j, :], y, oh[:, j, e:e + 1], tok[:, j, :],
                                                         ALU.mult, ALU.add)
                        if e == ET - 1 and r == 1:
                            ins.then_inc(combined, 1)
                        else:
                            done[r] = own.mark(ins)
                own.need(done[0])
                dve.wait_ge(combined, 2 * g + pr_ + 1)

            def shift(g):
                dve.wait_ge(rstd_ready, g + 1)
                js = slice(TPG * g, TPG * (g + 1))
                v.scalar_tensor_tensor(rstd[:, 2, js], mv[:, js, 0], -1.0, rstd[:, 0, js], ALU.mult, ALU.mult)\
                    .then_inc(shift_ready, 1)

            gates(0)
            mask(0)
            mask(1)
            for g in range(NG):
                combine(g, 0)
                if g == NG - 1:
                    shift(g - 1)
                combine(g, 1)
                moments(g).then_inc(var_ready, 1)
                if g == 0:
                    gates(1)
                    shift(0)
                if g + 2 < NG:
                    mask(g + 2)
                if g == 1:
                    shift(1)
            shift(NG - 1)

            def first_rest(p):
                dve.wait_ge(bc_ready, 2 * (p + 1))
                v.tensor_tensor(rest[:, :], bc[0:96, :], split[p % 2][:, :], ALU.subtract).then_inc(split_first, 1)

            def second_rest(p):
                dve.wait_ge(split_second, p + 1)
                v.tensor_copy(split[p % 2][32:64, :], part[32:64, :])
                own.link(v.tensor_tensor(rest[:, :], rest[:, :], part[:, :], ALU.subtract))
                v.tensor_copy(split[p % 2][64:96, :], rest[64:96, :]).then_inc(split_ready, 1)

            def normed(p):
                dve.wait_ge(rstd_psum, p + 1)
                v.tensor_tensor(two_banks(p), work[:, 1, :], two_banks(p), ALU.mult).then_inc(z_psum, 1)

            def residual(p):
                dve.wait_ge(z_scaled, p + 1)
                v.tensor_tensor(h_out(p), two_banks(p), h_in(p), ALU.add).then_inc(h_next, 1)

            dve.sem_inc(scanned, A_RING)
            first_rest(0)
            second_rest(0)
            dve.wait_ge(dt_parts, 1)
            own.link(v.tensor_tensor(dt[:, 0, :], work[:, 0, :], work[:, 1, :], ALU.add))
            v.tensor_tensor(du[:, 0, :], dt[:, 0, :], h_in(0), ALU.mult).then_inc(dt_ready, 1)
            for p in range(NPH):
                def pair(n, q, i, behind):
                    for r in range(2):
                        u = NS * p + n + r
                        dve.wait_ge(b_ready, u + 1)
                        v.tensor_tensor(bank(2 * r, 2), du[:, p % 2, :], bank(2 * r, 2), ALU.mult).then_inc(u_done, 1)
                    for r in range(2):
                        u = NS * p + n + r
                        dve.wait_ge(u_done, u + 1)
                        dve.wait_ge(a_ready, u + 1)
                        dve.wait_ge(g_ready, u + 1)
                        v.tensor_tensor_scan(h_ring[:, i + r, :], a_ring[:, i + r, :], bank(2 * r, 2), 0.0,
                                             ALU.mult, ALU.add).then_inc(scanned, 1)
                        if r == 0:
                            behind(n)

                dve.wait_ge(dt_ready, p + 1)
                pieces = {}
                if p > 0:
                    for n, piece in zip(DVE_POST, (normed, residual)):
                        pieces.setdefault(n, []).append(lambda piece=piece: piece(p - 1))
                if p + 1 < NPH:
                    for n, piece in zip(DVE_PREP, (first_rest, second_rest)):
                        pieces.setdefault(n, []).append(lambda piece=piece: piece(p + 1))
                units_of(dve, pieces, pair)
            normed(NPH - 1)
            own.link(v.tensor_tensor(tok[:, :, :], tok[:, :, :], bdec_bc[:, None, :].broadcast_to([P, NT, D]), ALU.add))
            residual(NPH - 1)
            for g in range(NG):
                js = slice(TPG * g, TPG * (g + 1))
                dve.wait_ge(dec_psum, g + 1)
                own.link(v.tensor_tensor(tok[:, js, :], bank(g % 2).rearrange("p (q d) -> p q d", d=D), tok[:, js, :],
                                         ALU.add))
                v.memset(idf[:, 1, 0:1], 0.0).then_inc(tok_done, 1)
                moments(g).then_inc(var2_ready, 1)
                if g:
                    normalise(g - 1, rstd2_ready).then_inc(z2_ready, 1)
            normalise(NG - 1, rstd2_ready).then_inc(z2_ready, 1)
            bc_e = lambda x: x[:, None, :].broadcast_to([P, NT, NE])
            bc_t = lambda x: x[:, :, None].broadcast_to([P, NT, NE])
            logits = bank(4)[:, 0:NT * NE].rearrange("p (j e) -> p j e", e=NE)
            dve.wait_ge(logits_ready, 1)
            own.link(v.tensor_tensor(lg[:, :, :], logits, bc_e(br_bc), ALU.add))
            own.link(v.tensor_reduce(rmax[:, 0, :], lg[:, :, :], AX.X, ALU.max))
            v.tensor_tensor(lg[:, :, :], lg[:, :, :], bc_t(rmax[:, 0, :]), ALU.subtract).then_inc(shifted, 1)
            dve.wait_ge(exped, 1)
            own.link(v.tensor_reduce(rmax[:, 1, :], pr[:, :, :], AX.X, ALU.add))
            own.link(v.reciprocal(rmax[:, 2, :], rmax[:, 1, :]))
            own.link(v.tensor_tensor(pr[:, :, :], pr[:, :, :], bc_t(rmax[:, 2, :]), ALU.mult))
            for j in range(NT):
                n = own.mark(v.max(m8[:, j, :], pr[:, j, :]))
            own.need(n)
            for j in range(NT):
                n = own.mark(v.max_index(i8[:, j, :], m8[:, j, :], pr[:, j, :]))
            own.need(n)
            own.link(v.tensor_copy(i8f[:, :, :], i8[:, :, 0:TOPK]))
            for k in range(TOPK):
                n = own.mark(v.tensor_tensor(ohk[k][:, :, :], bc_e(iota_e), bc_t(i8f[:, :, k]), ALU.is_equal))
            own.need(n)
            v.tensor_tensor(routed[:, :, :], ohk[0][:, :, :], ohk[1][:, :, :], ALU.add).then_inc(counted, 1)
            own.link(v.tensor_tensor(rmax[:, 3, :], m8[:, :, 0], m8[:, :, 1], ALU.add))
            own.link(v.tensor_scalar(rmax[:, 3, :], rmax[:, 3, :], 1e-9, None, ALU.add))
            own.link(v.reciprocal(rmax[:, 0, :], rmax[:, 3, :]))
            for k in range(TOPK):
                own.link(v.tensor_tensor(wk[:, k, :], m8[:, :, k], rmax[:, 0, :], ALU.mult))
            dve.wait_ge(pos_ready, 1)
            by_e = lambda x: x.rearrange("p (j e) -> p e j", e=NE)
            own.link(v.tensor_copy(cnt[:, :, :], by_e(bank(6)[:, 0:NT * NE])))
            own.link(v.tensor_tensor_scan(cum[:, :, :].rearrange("p e j -> p (e j)"),
                                          not_first[:, :, :].rearrange("p e j -> p (e j)"),
                                          cnt[:, :, :].rearrange("p e j -> p (e j)"), 0.0, ALU.mult, ALU.add))
            own.link(v.tensor_tensor(cum[:, :, :], cum[:, :, :], cnt[:, :, :], ALU.subtract))
            own.link(v.tensor_tensor(pos[:, :, :], bank(5)[:, 0:NT * NE].rearrange("p (j e) -> p j e", e=NE),
                                     cum[:, :, :].rearrange("p e j -> p j e"), ALU.add))
            own.link(v.tensor_tensor(slot[:, :, :], pos[:, :, :], bc_e(iota_cap), ALU.add))
            for k in range(TOPK):
                for src, dst in ((pos, posk), (slot, slotk)):
                    own.link(v.tensor_tensor(tmp[:, :, :], ohk[k][:, :, :], src[:, :, :], ALU.mult))
                    own.link(v.tensor_reduce(dst[:, k, :], tmp[:, :, :], AX.X, ALU.add))
            own.link(v.tensor_scalar(keep[:, :, :], posk[:, :, :], float(CAP), None, ALU.is_lt))
            own.link(v.tensor_scalar(posk[:, :, :], keep[:, :, :], -float(2 * ROWS), float(2 * ROWS), ALU.mult, ALU.add))
            own.link(v.tensor_tensor(posk[:, :, :], posk[:, :, :], slotk[:, :, :], ALU.add))
            v.tensor_copy(into[:, :, :], posk[:, :, :]).then_inc(idx_made, 1)
            own.link(v.tensor_scalar(slotk[:, :, :], slotk[:, :, :], float(ROWS - 1), None, ALU.min))
            v.tensor_copy(outof[:, :, :], slotk[:, :, :]).then_inc(idx_made, 1)
            own.link(v.tensor_tensor(wk[:, :, :], wk[:, :, :], keep[:, :, :], ALU.mult))
            own.link(v.tensor_tensor(rmax[:, 0, :], wk[:, 0, :], wk[:, 1, :], ALU.add))
            own.link(v.tensor_scalar(rmax[:, 0, :], rmax[:, 0, :], 1e-9, None, ALU.add))
            own.link(v.reciprocal(rmax[:, 1, :], rmax[:, 0, :]))
            for k in range(TOPK):
                own.link(v.tensor_tensor(wk[:, k, :], wk[:, k, :], rmax[:, 1, :], ALU.mult))
            dve.sem_inc(out_copied, OUT_RING)
            dve.wait_ge(xeT_ready, 1)
            v.tensor_copy(xeT[0], bank(4, 2)[:, 0:CAP]).then_inc(xeT_copied, 1)

            def rows_next(e, i):
                dve.wait_ge(xeT_ready, e + 1)
                v.tensor_copy(xeT[i], bank(4, 2)[:, 0:CAP]).then_inc(xeT_copied, 1)

            def output(e, i):
                dve.wait_ge(out_psum, e + 1)
                dve.wait_ge(rows_out[i], 8 * (e - i) + 16)
                v.tensor_tensor(ob[i], bank(6, 2)[:, 0:CAP].rearrange("p (t d) -> p t d", d=D),
                                b2_bc[:, bass.ds(e, 1), :].broadcast_to([P, ST, D]), ALU.add).then_inc(out_copied, 1)

            with dve.Fori(0, NE // 2 - 1) as k:
                for i in range(2):
                    e = 2 * k
                    rows_next(e + i + 1, 1 - i)
                    output(e + i, i)
            rows_next(NE - 1, 1)
            for i in range(2):
                output(NE - 2 + i, i)
            for g in range(NG):
                dve.wait_ge(got[g], 16 * TOPK * TPG)
                for k in range(TOPK):
                    for j in range(TPG * g, TPG * (g + 1)):
                        ins = v.scalar_tensor_tensor(out_sb[:, j, :], picked[k][:, j, :], wk[:, k, j:j + 1],
                                                     (tok if k == 0 else out_sb)[:, j, :], ALU.mult, ALU.add)
                        if k == 0:
                            n = own.mark(ins)
                        else:
                            ins.then_inc(out_ready, 1)
                    own.need(n)

        @block.tensor
        def _(pe):
            v = nc.tensor

            def mm(out_ap, lhsT, rhs, start=True, stop=True):
                return v.matmul(out_ap, lhsT, rhs, start=start, stop=stop)

            def wide(out_ap, lhsT, rhs, start=True, stop=True):
                for o, r in zip(halves(out_ap), halves(rhs)):
                    last = mm(o, lhsT, r, start, stop)
                return last

            pe.wait_ge(weights_in, 16 * N_LOADS)
            pe.wait_ge(filled, 1)
            mm(bank(0)[:, 0:NL], mean_w[:, :], cols[:, 2, :]).then_inc(bmix_mean, 1)

            def transpose_x(g):
                pe.wait_ge(masked, g + 1)
                if g > 0:
                    pe.wait_ge(xT_copied, g)
                for q in range(TPG):
                    last = v.transpose(bank(0)[:, q * P:(q + 1) * P], xm[g % 2][:, q, :], ident[:, :])
                last.then_inc(xT_ready, 1)

            def all_experts(g):
                pe.wait_ge(xT_copied, g + 1)
                for pr_ in range(2):
                    if g > 0:
                        pe.wait_ge(combined, 2 * (g - 1) + pr_ + 1)
                    b0 = 1 + 3 * pr_
                    for r in range(2):
                        x_ = xT[g % 2][:, (2 * pr_ + r) * P:(2 * pr_ + r + 1) * P]
                        for out_, es in ((bank(b0 + r), slice(0, 4)), (bank(b0 + 2)[:, r * D:(r + 1) * D], slice(4, 5))):
                            mm(out_, sel[0:96, 0, :], split[1][:, es.start * D:es.stop * D], True, False)
                            last = mm(out_, x_, tokw[:, es, :].rearrange("p e d -> p (e d)"), False, True)
                    last.then_inc(y_tok_ready, 1)

            def transpose_z(g):
                pe.wait_ge(z_ready, g + 1)
                if g > 0:
                    pe.wait_ge(hT_ready, g)
                for q in range(TPG):
                    last = v.transpose(bank(7)[:, q * P:(q + 1) * P], z[:, TPG * g + q, :], ident[:, :])
                last.then_inc(zT_ready, 1)

            pe.wait_ge(mean_ready, 1)
            pe.wait_ge(ident_ready, 1)
            pe.wait_ge(sel_ready, 1)
            pe.wait_ge(biases_ready, 1)
            pe.wait_ge(tok_in, 16)
            transpose_x(0)
            for g in range(NG):
                all_experts(g)
                if g + 1 < NG:
                    transpose_x(g + 1)
                if g > 0:
                    transpose_z(g - 1)
            transpose_z(NG - 1)

            def project_dt(p):
                if p > 0:
                    pe.wait_ge(bc_ready, 2 * (p + 1))
                wide(dt_banks(p), wdt[:, p // NSEQ, :], h_in(p)).then_inc(dt_psum, 1)

            def project_bc(p):
                if p >= NSEQ:
                    pe.wait_ge(h_next, p - NSEQ + 1)
                wide(two_banks(p), wbc[:, p // NSEQ, :], h_in(p)).then_inc(bc_psum, 1)

            def spread_b(p, n, r):
                pe.wait_ge(scanned, NS * p + n + 3)
                for h in range(2):
                    last = mm(bank(2 * r + h), sel[0:96, n, :], split[p % 2][:, h * HALF:(h + 1) * HALF])
                last.then_inc(b_ready, 1)

            def add_y(p, n):
                if n == 0:
                    pe.wait_ge(dt_parts, p + 1)
                    wide(two_banks(p), dskip[:, p // NSEQ, :], h_in(p), True, False)
                pe.wait_ge(g_ready, H_RING + NS * p + n + 1)
                wide(two_banks(p), ident[:, :], g_ring[:, n % GU, :], False, n == NS - 1).then_inc(y_added, 1)
                if n == NS - 1:
                    pe.wait_ge(y_added, G_RING + NS * (p + 1))
                    pe.sem_inc(y_ready, 1)

            def mix(p):
                pe.wait_ge(gelu_done, p + 1)
                wide(two_banks(p), wmix[:, p // NSEQ, :], work[:, 0, :]).then_inc(mixed, 1)

            def variance(p):
                pe.wait_ge(squared, p + 1)
                pe.wait_ge(centred, p + 1)
                wide(two_banks(p), mean_w[:, :], work[:, 0, :]).then_inc(var_psum, 1)

            pe.sem_inc(y_added, G_RING)
            pe.wait_ge(hT_ready, NG)
            pe.wait_ge(wbc_in, 16 * 8)
            pe.wait_ge(consts_ready, 1)
            project_bc(0)
            project_dt(0)
            pe.wait_ge(split_ready, 1)
            for r in range(2):
                spread_b(0, r, r)
            for p in range(NPH):
                pieces = {}
                if p > 0:
                    for n, piece in zip(PE_POST, (mix, variance)):
                        pieces.setdefault(n, []).append(lambda piece=piece: piece(p - 1))
                if p + 1 < NPH:
                    for n, piece in zip(PE_PREP, (project_bc, project_dt)):
                        pieces.setdefault(n, []).append(lambda piece=piece: piece(p + 1))
                for n in range(NS):
                    ahead, behind = NS * p + n + 2, NS * p + n - Y_LAG
                    if ahead < NS * NPH:
                        if ahead % NS == 0:
                            pe.wait_ge(split_ready, ahead // NS + 1)
                        spread_b(ahead // NS, ahead % NS, n % 2)
                    if behind >= 0:
                        add_y(behind // NS, behind % NS)
                    for piece in pieces.get(n, []):
                        piece()
            for n in range(NS - Y_LAG, NS):
                add_y(NPH - 1, n)
            mix(NPH - 1)
            variance(NPH - 1)
            pe.wait_ge(h_next, NPH)
            for g in range(NG):
                if g >= 2:
                    pe.wait_ge(tok_done, g - 1)
                for q in range(TPG):
                    j = TPG * g + q
                    last = mm(bank(g % 2)[:, q * D:(q + 1) * D], hT[NL % 2][:, j * P:(j + 1) * P], wdec[:, :])
                last.then_inc(dec_psum, 1)
            for g in range(NG):
                pe.wait_ge(z2_ready, g + 1)
                if g >= 2:
                    pe.wait_ge(z2T_copied, g - 1)
                for q in range(TPG):
                    last = v.transpose(bank(2 + g % 2)[:, q * P:(q + 1) * P], z[:, TPG * g + q, :], ident[:, :])
                last.then_inc(z2T_ready, 1)
                pe.wait_ge(z2T_copied, g + 1)
                for q in range(TPG):
                    j = TPG * g + q
                    last = mm(bank(4)[:, j * NE:(j + 1) * NE], work[:, g % 2, q * P:(q + 1) * P], wr[:, :])
            last.then_inc(logits_ready, 1)
            pe.wait_ge(counted, 1)
            r_ = routed[:, :, :].rearrange("p j e -> p (j e)")
            mm(bank(5)[:, 0:NT * NE], tri[:, :], r_)
            mm(bank(6)[:, 0:NT * NE], ones_bf[:, :], r_).then_inc(pos_ready, 1)

            def rows_in_(e, i):
                pe.wait_ge(rows_in[i], 8 * (e - i) + 16)
                for t in range(ST):
                    last = v.transpose(bank(4, 2)[:, t * P:(t + 1) * P], xb[i][:, t, :], ident[:, :])
                last.then_inc(xeT_ready, 1)

            def hidden(e, i):
                pe.wait_ge(xeT_copied, e + 1)
                pe.wait_ge(w_in[i], 16 * (e - i) + 32)
                for f in range(FC):
                    pe.wait_ge(hid_ready, FC * e + f + 1)
                    for h in range(2):
                        last = mm(bank(2 * (f % 2) + h)[:, 0:CAP // 2], w1b[i][:, f * P:(f + 1) * P],
                                  xeT[i][:, h * CAP // 2:(h + 1) * CAP // 2])
                    last.then_inc(hid_psum, 1)

            def outputs(e, i):
                pe.wait_ge(hid_ready, FC * e + FC + HID_RING)
                pe.wait_ge(out_copied, e + 1)
                for t in range(ST):
                    for f in range(FC):
                        last = mm(bank(6, 2)[:, t * D:(t + 1) * D], hid[:, f, t * P:(t + 1) * P], w2b[i][:, f, :],
                                  f == 0, f == FC - 1)
                last.then_inc(out_psum, 1)

            rows_in_(0, 0)
            with pe.Fori(0, NE // 2 - 1) as k:
                for i in range(2):
                    e = 2 * k
                    hidden(e + i, i)
                    rows_in_(e + i + 1, 1 - i)
                    outputs(e + i, i)
            hidden(NE - 2, 0)
            rows_in_(NE - 1, 1)
            outputs(NE - 2, 0)
            hidden(NE - 1, 1)
            outputs(NE - 1, 1)


def kernel(x, L0_tok_emb_table, L0_tok_gate_table, L0_tok_expert_w, L0_tok_expert_b, L0_attn_A_log, L0_attn_W_B,
           L0_attn_b_B, L0_attn_W_C, L0_attn_b_C, L0_attn_W_dt, L0_attn_b_dt, L0_attn_D_skip, L0_attn_W_mix,
           L0_attn_b_mix, L0_attn_ln_g, L0_attn_ln_b, L0_attn_W_dec, L0_attn_b_dec, L0_ffn_Wr, L0_ffn_br,
           L0_ffn_W1, L0_ffn_b1, L0_ffn_W2, L0_ffn_b2):
    import numpy as np
    import concourse.bacc as bacc
    from concourse import mybir as my
    from concourse.bass_utils import run_bass_kernel_spmd

    n = lambda a: np.asarray(a)
    B, S = n(x).shape
    E, D, F = n(L0_ffn_W1).shape
    feature_first = lambda a: n(a).swapaxes(0, 1)
    arrays = {
        "ids": n(x).reshape(-1, 128).T, "emb_gate": np.concatenate([n(L0_tok_emb_table), n(L0_tok_gate_table)], axis=1),
        "tok_w": n(L0_tok_expert_w).transpose(2, 0, 1),
        "tok_b": n(L0_tok_expert_b).reshape(1, -1),
        "A_log": feature_first(L0_attn_A_log), "W_B": feature_first(L0_attn_W_B), "b_B": n(L0_attn_b_B).T,
        "W_C": feature_first(L0_attn_W_C), "b_C": n(L0_attn_b_C).T, "W_dt": feature_first(L0_attn_W_dt),
        "b_dt": n(L0_attn_b_dt).T, "D_skip": n(L0_attn_D_skip).T, "W_mix": feature_first(L0_attn_W_mix),
        "b_mix": n(L0_attn_b_mix).T, "ln_g": n(L0_attn_ln_g).T, "ln_b": n(L0_attn_ln_b).T,
        "W_dec": n(L0_attn_W_dec), "b_dec": n(L0_attn_b_dec)[None, :], "Wr": n(L0_ffn_Wr),
        "br": n(L0_ffn_br)[None, :], "W1": n(L0_ffn_W1).transpose(1, 0, 2),
        "b1": n(L0_ffn_b1).reshape(E, F // 128, 128).transpose(2, 0, 1),
        "W2": n(L0_ffn_W2).reshape(E, F // 128, 128, D).transpose(2, 0, 1, 3).reshape(128, E, F // 128 * D),
        "b2": n(L0_ffn_b2)[None, :, :],
    }
    arrays = {k: np.ascontiguousarray(a) for k, a in arrays.items()}
    nc = bacc.Bacc("TRN2", target_bir_lowering=False, num_devices=1)
    args = [nc.dram_tensor("in_" + k, a.shape, my.dt.from_np(a.dtype), kind="ExternalInput").ap()
            for k, a in arrays.items()]
    out = nc.dram_tensor("out", [128, B * S // 128, D], my.dt.float32, kind="ExternalOutput").ap()
    tower_kernel(nc, *args, out)
    r = run_bass_kernel_spmd(nc, [{"in_" + k: a for k, a in arrays.items()}], core_ids=[0])
    got = r.results[0]["out"]
    return got.transpose(1, 0, 2).reshape(B, S, D)
```

```python
import concourse.bass as bass
from concourse import mybir
from contextlib import ExitStack

F32, BF16 = mybir.dt.float32, mybir.dt.bfloat16
I32, U32 = mybir.dt.int32, mybir.dt.uint32
ALU = mybir.AluOpType
ACT = mybir.ActivationFunctionType
AX = mybir.AxisListType


class Chain:

    def __init__(self, engine, semaphore):
        self.engine, self.semaphore, self.count = engine, semaphore, 0

    def mark(self, instruction):
        instruction.then_inc(self.semaphore, 1)
        self.count += 1
        return self.count

    def need(self, count):
        self.engine.wait_ge(self.semaphore, count)

    def link(self, instruction):
        self.need(self.mark(instruction))


def tower_kernel(nc, ids, emb_gate, tok_w, tok_b, A_log, W_B, b_B, W_C, b_C, W_dt, b_dt,
                 D_skip, W_mix, b_mix, ln_g, ln_b, W_dec, b_dec, Wr, br, W1, b1, W2, b2, out):
    P = 128
    VOCAB, D = emb_gate.shape[0], emb_gate.shape[1] - 1
    NT = ids.shape[1]
    T = NT * P
    NSEQ, L = 2, T // 2
    NL = A_log.shape[1]
    NS = A_log.shape[2]
    ET = tok_w.shape[1]
    NE = Wr.shape[1]
    FF = W1.shape[2]
    FC = FF // P
    TOPK = 2
    CAP = -(-5 * T * TOPK // (4 * NE))
    ROWS = NE * CAP
    ST = CAP // P
    HALF = 512
    NSPLIT = L // HALF
    TPG = HALF // D
    NG = NT // TPG
    NPH = NL * NSEQ
    GU = 4
    NQ = NS // GU
    EPS = 1e-5
    STEP = D // ET
    EXACT = float(2 ** 23)
    FAR = 4 * T
    TPS = NT // NSEQ
    ROUTED = (range(TPS), *(range(j, j + TPG) for j in range(TPS, NT, TPG)))
    N_LOADS = 14
    assert ROWS % P == 0 and CAP % P == 0 and NSPLIT * NS == 32

    x_rows = nc.dram_tensor("x_rows", [ROWS, D + 2], F32, kind="Internal").ap()
    y_tok = nc.dram_tensor("y_tok", [TOPK * T, D], F32, kind="Internal").ap()
    c_dram = nc.dram_tensor("c_dram", [NPH, NSPLIT, NS, HALF], F32, kind="Internal").ap()

    ctx = ExitStack()
    with ctx:
        def sb(name, shape, dt=F32):
            return ctx.enter_context(nc.sbuf_tensor(name, shape, dt))

        def sem(name):
            return ctx.enter_context(nc.semaphore(name))

        ident = sb("ident", [P, P])
        iota_d = sb("iota_d", [P, P])
        sel = sb("sel", [P, NSPLIT * NS, P], BF16)
        tri = sb("tri", [P, P], BF16)
        ones_bf = sb("ones_bf", [P, P], BF16)
        mean_w = sb("mean_w", [P, P])
        iota_e = sb("iota_e", [P, NE])
        iota_cap = sb("iota_cap", [P, NE])
        not_first = sb("not_first", [P, NE, NT])
        eps_col = sb("eps_col", [P, 1])
        one_col = sb("one_col", [P, 1])
        tokw = sb("tokw", [P, ET, D])
        negA = sb("negA", [P, NL, NS])
        wbc = sb("wbc", [P, NL, NSPLIT, P])
        bbc = sb("bbc", [P, NL])
        wdt = sb("wdt", [P, NL, D])
        wmix = sb("wmix", [P, NL, D])
        cols = sb("cols", [P, 5, NL])
        wdec = sb("wdec", [P, D])
        bdec_bc = sb("bdec_bc", [P, D])
        wr = sb("wr", [P, NE])
        br_bc = sb("br_bc", [P, NE])
        b1_sb = sb("b1_sb", [P, NE, FC])
        b2_bc = sb("b2_bc", [P, NE, D])
        ids_sb = sb("ids_sb", [P, NT], I32)
        idf = sb("idf", [P, 2, NT])
        idx = sb("idx", [P, NT], U32)
        gate = sb("gate", [P, 5, NT])
        gate_i = sb("gate_i", [P, NT], I32)
        ge = sb("ge", [P, NT, ET - 1])
        oh = sb("oh", [P, NT, ET])
        tok = sb("tok", [P, NT, D])
        stats = sb("stats", [P, NT, 6])
        mv = sb("mv", [P, NT, 2])
        rstd = sb("rstd", [P, 3, NT])
        hT = [sb(f"hT{i}", [P, T]) for i in range(2)]
        dt = sb("dt", [P, 2, L])
        du = sb("du", [P, 2, L])
        bc = sb("bc", [P, L])
        rest = sb("rest", [96, ET * D])
        part = sb("part", [96, ET * D], BF16)
        split = [sb(f"split{i}", [96, ET * D], BF16) for i in range(2)]
        a_ring = sb("a_ring", [P, GU, L])
        h_ring = sb("h_ring", [P, GU, L])
        g_ring = sb("g_ring", [P, GU, L])
        work = sb("work", [P, 2, L])
        big = sb("big", [P, NS, L])
        z = h_ring[:, 2:4, :].rearrange("p a b -> p (a b)").rearrange("p (j d) -> p j d", d=D)
        out_sb = h_ring[:, 0:2, :].rearrange("p a b -> p (a b)").rearrange("p (j d) -> p j d", d=D)

        ps = ctx.enter_context(nc.psum_tensor("ps", [P, 8 * HALF], F32))

        def bank(i, n=1):
            return ps[:, i * HALF:(i + n) * HALF]

        emb = big[:, 0:3, :].rearrange("p a b -> p (a b)")[:, 0:NT * (D + 1)].rearrange("p (j d) -> p j d", d=D + 1)
        mk = [big[:, 14, i * HALF:(i + 1) * HALF].rearrange("p (q d) -> p q d", d=D) for i in range(2)]
        xm = [big[:, 3, i * HALF:(i + 1) * HALF].rearrange("p (q d) -> p q d", d=D) for i in range(2)]
        xT = [big[:, 15, i * HALF:(i + 1) * HALF] for i in range(2)]
        zero = big[:, 4:14, :].rearrange("p a b -> p (a b)")[:, 0:ROWS * (D + 2) // P]
        flat = big[:, :, :].rearrange("p a b -> p (a b)")
        z2 = flat[:, 0:NT * (D + 2)].rearrange("p (j c) -> p j c", c=D + 2)
        o0 = 3 * L
        w1b = [flat[:, o0 + i * FF:o0 + (i + 1) * FF] for i in range(2)]
        w2b = [flat[:, o0 + (2 + i) * FF:o0 + (3 + i) * FF].rearrange("p (c d) -> p c d", d=D) for i in range(2)]
        o1, XW = o0 + 4 * FF, ST * (D + 2)
        xb = [flat[:, o1 + i * XW:o1 + (i + 1) * XW].rearrange("p (t c) -> p t c", c=D + 2) for i in range(2)]
        o2 = o1 + 2 * XW
        xeT = [flat[:, o2 + i * CAP:o2 + (i + 1) * CAP] for i in range(2)]
        ob = [flat[:, o2 + (2 + i) * CAP:o2 + (3 + i) * CAP].rearrange("p (t d) -> p t d", d=D) for i in range(2)]
        o3 = o2 + 4 * CAP
        hid = [flat[:, o3 + i * FC * CAP:o3 + (i + 1) * FC * CAP].rearrange("p (f c) -> p f c", f=FC) for i in range(2)]
        picked = [a_ring[:, 2 * k:2 * k + 2, :].rearrange("p a b -> p (a b)").rearrange("p (j d) -> p j d", d=D)
                  for k in range(TOPK)]
        lg = sb("lg", [P, NT, NE])
        pr = sb("pr", [P, NT, NE])
        rmax = sb("rmax", [P, 4, NT])
        m8 = sb("m8", [P, NT, 8])
        i8 = sb("i8", [P, NT, 8], U32)
        i8f = sb("i8f", [P, NT, TOPK])
        ohk = [sb(f"ohk{k}", [P, NT, NE]) for k in range(TOPK)]
        routed = sb("routed", [P, NT, NE], BF16)
        cnt = sb("cnt", [P, NE, NT])
        cum = sb("cum", [P, NE, NT])
        pos = sb("pos", [P, NT, NE])
        slot = sb("slot", [P, NT, NE])
        tmp4 = [sb(f"tmp{i}", [P, NT // 2, NE]) for i in range(4)]
        wk = sb("wk", [P, TOPK, NT])
        posk = sb("posk", [P, TOPK, NT])
        keep = sb("keep", [P, TOPK, NT])
        slotk = sb("slotk", [P, TOPK, NT])
        into = sb("into", [P, TOPK, NT], U32)
        is_second = sb("is_second", [P, ST])
        dest = sb("dest", [P, ST])
        dest_i = [sb(f"dest_i{i}", [P, ST], U32) for i in range(2)]

        (ids_in, tok_in, weights_in, wbc_in, wbc_zero, idx_ready, consts_ready, zero_ready, zeroed, negA_ready,
         filled, gates_ready, ident_ready, sel_ready, biases_zero, shift_ready,
         mean_ready, bmix_mean, folded, xT_ready, xT_copied, biases_in, biases_ready,
         y_tok_ready, first_taken, combined, var_ready, rstd_ready, z_ready, zT_ready, hT_ready,
         dt_psum, relu_done, dt_parts, dt_ready, bc_psum, bc_ready, c_stored, split_first, split_second, split_ready,
         b_ready, a_ready, skip_ready, skip_added, u_done, scanned, g_ready, y_added, y_ready, gelu_done, mixed, squared, centred, var_psum,
         rstd_psum, z_psum, h_next, bdec_added, dec_psum, tok_done, var2_ready, rstd2_ready, origin_ready, z2_ready,
         z2T_ready, z2T_copied, logits_ready, shifted, exped, counted, pos_ready, idx_made, scattered,
         xeT_ready, xeT_copied, hid_psum, hid_ready, out_psum, out_copied, second_ready, dest_sum, dest_ready, weighted, out_ready, out_last, out_stored,
         chain_dve, chain_pool, chain_act) = [sem(name) for name in """
            ids_in tok_in weights_in wbc_in wbc_zero idx_ready consts_ready zero_ready zeroed negA_ready
            filled gates_ready ident_ready sel_ready biases_zero shift_ready
            mean_ready bmix_mean folded xT_ready xT_copied biases_in biases_ready
            y_tok_ready first_taken combined var_ready rstd_ready z_ready zT_ready hT_ready
            dt_psum relu_done dt_parts dt_ready bc_psum bc_ready c_stored split_first split_second split_ready
            b_ready a_ready skip_ready skip_added u_done scanned g_ready y_added y_ready gelu_done mixed squared centred var_psum
            rstd_psum z_psum h_next bdec_added dec_psum tok_done var2_ready rstd2_ready origin_ready z2_ready
            z2T_ready z2T_copied logits_ready shifted exped counted pos_ready idx_made scattered
            xeT_ready xeT_copied hid_psum hid_ready out_psum out_copied second_ready dest_sum dest_ready weighted out_ready out_last out_stored
            chain_dve chain_pool chain_act""".split()]
        masked = [sem(f"masked{i}") for i in range(NSEQ)]
        emb_in = [sem(f"emb_in{i}") for i in range(NSEQ)]
        c_in = [sem(f"c_in{k}") for k in range(NS // 2)]
        w_in = [sem(f"w_in{i}") for i in range(2)]
        rows_in = [sem(f"rows_in{i}") for i in range(2)]
        rows_out, outputs_free = sem("rows_out"), sem("outputs_free")
        got = [sem(f"got{g}") for g in range(NG)]
        block = ctx.enter_context(nc.Block())

        def halves(ap):
            return [ap[:, h * HALF:(h + 1) * HALF] for h in range(2)]


        def part_of(ap, h):
            return ap if h is None else halves(ap)[h]

        def count(p, h):
            return p + 1 + (h or 0)

        def tokens(p):
            return slice((p % NSEQ) * L, (p % NSEQ + 1) * L)

        def h_in(p):
            return hT[p // NSEQ % 2][:, tokens(p)]

        def h_out(p):
            return hT[(p // NSEQ + 1) % 2][:, tokens(p)]

        def bc_banks(p):
            return two_banks(p)[:, 0:HALF] if p else bank(0)

        def dt_banks(p):
            return two_banks(p) if p else bank(2, 2)

        def decoded_bank(g):
            return bank((4, 5, 0, 1)[g])

        def z2T_bank(g):
            return bank((4, 5, 2, 3)[g])

        logits_bank, count_bank = bank(4), bank(5)

        def units_of(engine, pieces, pair):
            def behind(n):
                for piece in pieces.get(n, []) if isinstance(n, int) else []:
                    piece()

            for q in range(NQ):
                n0 = GU * q
                if any(n in pieces for n in range(n0, n0 + GU - 1)):
                    for i in range(0, GU, 2):
                        pair(n0 + i, q, i, behind)
                        behind(n0 + i + 1)
                else:
                    with engine.Fori(0, GU // 2) as k:
                        pair(2 * k + n0, q, 2 * k, behind)
                    behind(n0 + GU - 1)

        H_RING, A_RING, G_RING = GU, GU, GU
        HID_RING, OUT_RING = 2, 2
        Y_LAG = 3
        SKIP_UNIT = 2
        PE_POST = (7, 7, 10, 10)
        PE_PREP = (18, 19, 22, 23)
        ACT_POST = (4, 6, 8)
        ACT_PREP = (12, 13, 15)
        DVE_POST = (7, 8)
        DVE_PREP = (11, 12, 14)
        PE_ROUTER = (21, 31, 31)
        ACT_ROUTER = (14, 14)
        DVE_ROUTER = (12, 12)

        def two_banks(p):
            return bank(4 + 2 * (p % 2), 2)

        PARTS = ((0, ST // 2), (ST // 2, ST))

        def part_psum(a):
            return bank(6 + a)[:, 0:(PARTS[a][1] - PARTS[a][0]) * D].rearrange("p (t d) -> p t d", d=D)

        def mask(v, own, g):
            buffer = mk[g // 2]
            if g % 2:
                own.engine.wait_ge(masked[g // 2], 1)
            if g >= 2:
                own.engine.wait_ge(xT_ready, g - 1)
            for q in range(TPG):
                j = TPG * g + q
                own.mark(v.tensor_scalar(buffer[:, q, :], iota_d[:, :], gate[:, 0, j:j + 1],
                                         gate[:, 4, j:j + 1], ALU.is_lt, ALU.add))
            own.need(own.count)
            for q in range(TPG):
                last = v.tensor_tensor(xm[g % 2][:, q, :], emb[:, TPG * g + q, 0:D], buffer[:, q, :], ALU.mult)
            last.then_inc(masked[g // 2], 1)

        @block.sync
        def _(sp):
            sp.dma_start(ids_sb[:, :], ids).then_inc(ids_in, 16)
            sp.dma_start(tokw[:, :, :], tok_w).then_inc(tok_in, 16)
            sp.wait_ge(biases_zero, 1)
            for i in range(3):
                sp.dma_start(bc[32 * i:32 * i + 1, 0:ET * D], tok_b).then_inc(biases_in, 16)
            loads = [(wmix[:, :, :], W_mix), (negA[:, :, :], A_log), (wdt[:, :, :], W_dt),
                     (wdec[:, :], W_dec), (wr[:, :], Wr), (b1_sb[:, :, :], b1),
                     (bdec_bc[:, :], b_dec.broadcast_to([P, D])), (br_bc[:, :], br.broadcast_to([P, NE])),
                     (b2_bc[:, :, :], b2.broadcast_to([P, NE, D]))]
            loads += [(cols[:, i, :], c) for i, c in enumerate((b_dt, D_skip, b_mix, ln_g, ln_b))]
            assert len(loads) == N_LOADS
            for dst, src in loads:
                sp.dma_start(dst, src).then_inc(weights_in, 16)
            sp.wait_ge(wbc_zero, 2)
            for i, (w, b) in enumerate(((W_B, b_B), (W_B, b_B), (W_B, b_B), (W_C, b_C))):
                for h in range(NSPLIT):
                    c = 32 * i + NS * h
                    sp.dma_start(wbc[:, :, h, c:c + NS], w).then_inc(wbc_in, 16)
                    sp.dma_start(bbc[c:c + NS, :], b).then_inc(wbc_in, 16)
            sp.wait_ge(zero_ready, 1)
            sp.wait_ge(emb_in[1], 16 * NT // NSEQ)
            sp.dma_start(x_rows.rearrange("(p n) d -> p (n d)", p=P), zero).then_inc(zeroed, 16)
            sp.dma_start(y_tok.rearrange("(p n) d -> p (n d)", p=P), zero[:, 0:TOPK * T * D // P]).then_inc(zeroed, 16)
            for p in range(NPH):
                sp.wait_ge(bc_ready, 2 * p + 1)
                sp.dma_start(c_dram[p].rearrange("h n l -> (h n) l"), bc[96:P, 0:HALF]).then_inc(c_stored, 16)
                sp.wait_ge(c_stored, 16 * (p + 1))
                if p == 0:
                    sp.wait_ge(y_tok_ready, 2 * NG)
                    sp.wait_ge(zeroed, 16 * 2)
                for k in range(NS // 2):
                    if p > 0:
                        sp.wait_ge(g_ready, H_RING + NS * (p - 1) + 2 * (k + 1))
                    for h in range(NSPLIT):
                        sp.dma_start(big[:, 2 * k:2 * k + 2, h * HALF:(h + 1) * HALF],
                                     c_dram[p, h:h + 1, 2 * k:2 * k + 2, :].broadcast_to([P, 2, HALF]))\
                            .then_inc(c_in[k], 16)

            rows_v = x_rows.rearrange("(e t p) c -> p e t c", p=P, e=NE)
            y_v = y_tok.rearrange("(k j p) d -> p k j d", p=P, k=TOPK)

            def load_weights(e, i):
                sp.dma_start(w1b[i], W1[:, e, :]).then_inc(w_in[i], 16)
                sp.dma_start(w2b[i].rearrange("p c d -> p (c d)"), W2[:, e, :]).then_inc(w_in[i], 16)

            def load_rows(e, i):
                sp.dma_start(xb[i], rows_v[:, e, :, :]).then_inc(rows_in[i], 16)

            sp.wait_ge(g_ready, H_RING + NS * NPH)
            for i in range(2):
                load_weights(i, i)
            sp.wait_ge(scattered, 16 * TOPK * NT)
            for i in range(2):
                load_rows(i, i)
            with sp.Fori(0, NE // 2 - 1) as k:
                for i in range(2):
                    e = 2 * k
                    sp.wait_ge(xeT_ready, e + i + 1)
                    sp.wait_ge(dest_ready, e + i + 1)
                    load_rows(e + i + 2, i)
                    sp.wait_ge(out_psum, 2 * e + 2 * (i + 1))
                    load_weights(e + i + 2, i)
            sp.wait_ge(rows_out, 16 * ST * NE)
            for g in (0, NG - 1, *range(1, NG - 1)):
                js = slice(TPG * g, TPG * (g + 1))
                for k in range(TOPK):
                    sp.dma_start(picked[k][:, js, :], y_v[:, k, js, :]).then_inc(got[g], 16)
            for g in range(NG):
                if g < NG - 1:
                    sp.wait_ge(out_ready, TPG * (g + 1))
                else:
                    sp.wait_ge(out_last, 1)
                js = slice(TPG * g, TPG * (g + 1))
                sp.dma_start(out[:, js, :], out_sb[:, js, :]).then_inc(out_stored, 16)
            sp.wait_ge(out_stored, 16 * NG)

        @block.gpsimd
        def _(pool):
            v = nc.gpsimd
            own = Chain(pool, chain_pool)
            v.iota(iota_d[:, :], [[1, P]], 0, 0, allow_small_or_imprecise_dtypes=True)
            own.link(v.memset(ident[:, :], 0.0))
            v.affine_select(ident[:, :], ident[:, :], [[-1, P]], ALU.not_equal, 1.0, 0, 1).then_inc(ident_ready, 1)

            def gather(h):
                for j in range(h * NT // NSEQ, (h + 1) * NT // NSEQ):
                    v.indirect_dma_start(emb[:, j, :], None, emb_gate,
                                         bass.IndirectOffsetOnAxis(ap=idx[:, j:j + 1], axis=0)).then_inc(emb_in[h], 16)

            def select_rows(n0, n1, k):
                part_ = sel[:, n0:n1, :]
                return v.affine_select(part_, part_, [[-1, n1 - n0], [0, P]], ALU.not_equal, 1.0, -32 * k - n0, 1)

            pool.wait_ge(idx_ready, 1)
            gather(0)
            pool.wait_ge(filled, 1)
            own.link(select_rows(0, 1, 0))
            own.link(select_rows(0, 1, 1))
            select_rows(0, 1, 2).then_inc(sel_ready, 1)
            gather(1)
            pool.wait_ge(gates_ready, 2)
            for g in range(NG // 2, NG):
                mask(v, own, g)
            v.memset(zero, 0.0).then_inc(zero_ready, 1)
            for k in range(3):
                own.link(select_rows(1, NSPLIT * NS, k))
            v.affine_select(tri[:, :], ones_bf[:, :], [[1, P]], ALU.is_gt, 0.0, 0, -1)
            v.iota(iota_e[:, :], [[1, NE]], 0, 0, allow_small_or_imprecise_dtypes=True)
            v.iota(iota_cap[:, :], [[CAP, NE]], 0, 0, allow_small_or_imprecise_dtypes=True).then_inc(consts_ready, 1)

            def add_skip(p):
                pool.wait_ge(skip_ready, p + 1)
                pool.wait_ge(g_ready, H_RING + NS * p + SKIP_UNIT + 1)
                slot_ = g_ring[:, SKIP_UNIT % GU, :]
                v.tensor_tensor(slot_, slot_, bc[:, :], ALU.add).then_inc(skip_added, 1)

            pool.sem_inc(g_ready, H_RING)
            for p in range(NPH):
                def product(n):
                    u = NS * p + n
                    if n % 2 == 0:
                        pool.wait_ge(c_in[n // 2], 16 * NSPLIT * (p + 1))
                    pool.wait_ge(scanned, A_RING + u + 1)
                    pool.wait_ge(y_added, u + 1)
                    v.tensor_tensor(g_ring[:, n % GU, :], h_ring[:, n % GU, :], big[:, n, :], ALU.mult)\
                        .then_inc(g_ready, 1)

                for n in range(NS):
                    product(n)
                    if n == SKIP_UNIT + 1:
                        add_skip(p)
            pool.wait_ge(g_ready, H_RING + NS * NPH)
            v.iota(z2[:, :, D], [[P, NT]], -FAR, 1, allow_small_or_imprecise_dtypes=True).then_inc(origin_ready, 1)
            pool.wait_ge(origin_ready, 1)
            pool.wait_ge(zeroed, 16 * 2)
            pool.sem_inc(outputs_free, 2)
            for r, tiles in enumerate(ROUTED):
                pool.wait_ge(idx_made, r + 1)
                for k in range(TOPK):
                    for j in tiles:
                        v.indirect_dma_start(x_rows, bass.IndirectOffsetOnAxis(ap=into[:, k, j:j + 1], axis=0),
                                             z2[:, j, :], None, bounds_check=ROWS - 1, oob_is_err=False)\
                            .then_inc(scattered, 16)
            for e in range(NE):
                if e > 0:
                    pool.wait_ge(rows_out, 16 * ST * e)
                    pool.sem_inc(outputs_free, 1)
                pool.wait_ge(dest_ready, e + 1)
                for t in range(ST):
                    if t in (PARTS[0][0], PARTS[1][0]):
                        pool.wait_ge(out_copied, OUT_RING + 2 * e + (t > 0) + 1)
                    v.indirect_dma_start(y_tok, bass.IndirectOffsetOnAxis(ap=dest_i[e % 2][:, t:t + 1], axis=0),
                                         ob[e % 2][:, t, :], None, bounds_check=TOPK * T - 1, oob_is_err=False)\
                        .then_inc(rows_out, 16)
            js = slice(TPG * (NG - 1), NT)
            pool.wait_ge(weighted, 1)
            own.link(v.tensor_tensor(out_sb[:, js, :], tok[:, js, :], picked[0][:, js, :], ALU.add))
            pool.wait_ge(weighted, 2)
            v.tensor_tensor(out_sb[:, js, :], out_sb[:, js, :], picked[1][:, js, :], ALU.add).then_inc(out_last, 1)

        @block.scalar
        def _(act):
            v = nc.scalar
            own = Chain(act, chain_act)
            v.preload_act_table_set("natural_log_exp_and_others")
            act.wait_ge(weights_in, 16 * N_LOADS)
            own.link(v.activation(negA[:, :, :], negA[:, :, :], ACT.Exp))
            v.activation(negA[:, :, :], negA[:, :, :], ACT.Copy, scale=-1.0).then_inc(negA_ready, 1)

            def reciprocal_root(dst, var, tmp):
                own.link(v.activation(tmp, var, ACT.Ln, bias=eps_col[:, :]))
                return v.activation(dst, tmp, ACT.Exp, scale=-0.5)

            def copy_xT(g):
                act.wait_ge(xT_ready, g + 1)
                if g >= 2:
                    act.wait_ge(y_tok_ready, 2 * (g - 1))
                v.activation(xT[g % 2], bank(0), ACT.Copy).then_inc(xT_copied, 1)

            def normalise(g):
                js = slice(TPG * g, TPG * (g + 1))
                act.wait_ge(var_ready, g + 1)
                reciprocal_root(rstd[:, 0, js], mv[:, js, 1], rstd[:, 1, js]).then_inc(rstd_ready, 1)
                act.wait_ge(shift_ready, g + 1)
                for j in range(TPG * g, TPG * (g + 1)):
                    last = v.activation(z[:, j, :], tok[:, j, :], ACT.Identity, bias=rstd[:, 2, j:j + 1],
                                        scale=rstd[:, 0, j:j + 1])
                last.then_inc(z_ready, 1)

            def copy_hT(g):
                act.wait_ge(zT_ready, g + 1)
                v.activation(hT[0][:, HALF * g:HALF * (g + 1)], bank(7), ACT.Copy).then_inc(hT_ready, 1)

            def take_first(g, pr_):
                act.wait_ge(gates_ready, g // 2 + 1)
                act.wait_ge(y_tok_ready, 2 * g + pr_ + 1)
                for r in range(2):
                    j = TPG * g + 2 * pr_ + r
                    last = v.activation(tok[:, j, :], bank(1 + 3 * pr_ + r)[:, 0:D], ACT.Copy, scale=oh[:, j, 0:1])
                last.then_inc(first_taken, 1)

            copy_xT(0)
            for g in range(NG):
                take_first(g, 0)
                if g + 1 < NG:
                    copy_xT(g + 1)
                take_first(g, 1)
                if g > 0:
                    normalise(g - 1)
                if g > 1:
                    copy_hT(g - 2)
            normalise(NG - 1)

            def abs_and_relu(p):
                l = p // NSEQ
                act.wait_ge(dt_psum, p + 1)
                own.mark(v.activation(work[:, 0, :], dt_banks(p), ACT.Abs, bias=cols[:, 0, l:l + 1]))
                v.activation(work[:, 1, :], dt_banks(p), ACT.Relu, bias=cols[:, 0, l:l + 1]).then_inc(relu_done, 1)

            def log_part(p):
                own.need(own.count)
                own.link(v.activation(work[:, 0, :], work[:, 0, :], ACT.Exp, scale=-1.0))
                v.activation(work[:, 0, :], work[:, 0, :], ACT.Ln, bias=one_col[:, :]).then_inc(dt_parts, 1)

            def softplus_parts(p):
                abs_and_relu(p)
                log_part(p)

            def b_and_c(p):
                l = p // NSEQ
                act.wait_ge(bc_psum, p + 1)
                if p > 0:
                    act.wait_ge(skip_added, p)
                v.activation(bc[:, 0:HALF], bc_banks(p), ACT.Identity, bias=bbc[:, l:l + 1]).then_inc(bc_ready, 1)
                v.activation(split[p % 2][:, 0:HALF], bc_banks(p)[0:96, :], ACT.Identity, bias=bbc[0:96, l:l + 1])\
                    .then_inc(bc_ready, 1)

            def second_part(p):
                act.wait_ge(split_first, p + 1)
                v.activation(part[64:96, 0:HALF], rest[64:96, 0:HALF], ACT.Copy).then_inc(split_second, 1)
                v.activation(split[p % 2][32:64, 0:HALF], rest[32:64, 0:HALF], ACT.Copy).then_inc(split_ready, 1)

            def skip(p):
                act.wait_ge(c_stored, 16 * (p + 1))
                act.wait_ge(split_ready, 2 * (p + 1))
                v.activation(bc[:, :], h_in(p), ACT.Copy, scale=cols[:, 1, p // NSEQ:p // NSEQ + 1])\
                    .then_inc(skip_ready, 1)

            def gelu(p, h=None):
                act.wait_ge(y_ready, p + 1)
                v.activation(part_of(work[:, 0, :], h), part_of(two_banks(p), h), ACT.Gelu).then_inc(gelu_done, 1)
                if h != 0:
                    v.preload_act_table_set("natural_log_exp_and_others")

            def centre(p, h=None):
                bias = cols[:, 2, p // NSEQ:p // NSEQ + 1]
                y = part_of(two_banks(p), h)
                act.wait_ge(mixed, count(p, h))
                v.activation(part_of(work[:, 0, :], h), y, ACT.Square, bias=bias).then_inc(squared, 1)
                v.activation(part_of(work[:, 1, :], h), y, ACT.Identity, bias=bias).then_inc(centred, 1)

            def root(p, h=None):
                y = part_of(two_banks(p), h)
                act.wait_ge(var_psum, count(p, h))
                reciprocal_root(y, y, y).then_inc(rstd_psum, 1)

            def deviation(g):
                js = slice(TPG * g, TPG * (g + 1))
                act.wait_ge(var2_ready, g + 1)
                reciprocal_root(rstd[:, 0, js], mv[:, js, 1], rstd[:, 1, js]).then_inc(rstd2_ready, 1)

            def copy_z2T(g):
                act.wait_ge(z2T_ready, g + 1)
                if g == NG // 2:
                    act.wait_ge(logits_ready, 1)
                v.activation(work[:, g % 2, 0:HALF], z2T_bank(g), ACT.Copy).then_inc(z2T_copied, 1)

            def exp_logits(r):
                js = slice(ROUTED[r].start, ROUTED[r].stop)
                act.wait_ge(shifted, r + 1)
                v.activation(pr[:, js, :], lg[:, js, :], ACT.Exp).then_inc(exped, 1)

            b_and_c(0)
            abs_and_relu(0)
            second_part(0)
            log_part(0)
            for g in range(NG - 2, NG):
                copy_hT(g)
            for p in range(NPH):
                def pair(n, q, i, behind):
                    for r in range(2):
                        u = NS * p + n + r
                        act.wait_ge(scanned, u + 1)
                        nn = n + r
                        v.activation(a_ring[:, i + r, :], dt[:, p % 2, :], ACT.Exp,
                                     scale=negA[:, p // NSEQ, bass.ds(nn, 1)]).then_inc(a_ready, 1)
                        if r == 0:
                            behind(n)

                skip(p)
                act.wait_ge(dt_ready, p + 1)
                pieces = {}
                if p > 0:
                    for n, piece in zip(ACT_POST, (gelu, centre, root)):
                        pieces.setdefault(n, []).append(lambda piece=piece: piece(p - 1))
                if p + 1 == NPH:
                    pieces.setdefault(ACT_ROUTER[0], []).append(lambda: [deviation(g) for g in range(NG // 2)])
                    pieces.setdefault(ACT_ROUTER[1], []).append(lambda: [copy_z2T(g) for g in range(NG // 2)])
                if p + 1 < NPH:
                    for n, piece in zip(ACT_PREP, (b_and_c, second_part, softplus_parts)):
                        pieces.setdefault(n, []).append(lambda piece=piece: piece(p + 1))
                units_of(act, pieces, pair)
            last = NPH - 1
            exp_logits(0)
            for piece in (gelu, centre, root):
                for h in range(2):
                    piece(last, h)
            for g in range(NG // 2, NG):
                deviation(g)
            for g in range(NG // 2, NG):
                copy_z2T(g)
            for r in range(1, len(ROUTED)):
                exp_logits(r)
            act.sem_inc(hid_ready, HID_RING)
            v.preload_act_table_set("gelu_and_others")
            with act.Fori(0, NE // 2) as k:
                for i in range(2):
                    for f in range(FC):
                        act.wait_ge(hid_psum, 2 * FC * k + FC * i + f + 1)
                        v.activation(hid[i][:, f, :].rearrange("p (a b) -> p a b", a=2),
                                     bank(2 * (f % 2), 2).rearrange("p (a b) -> p a b", a=2)[:, :, 0:CAP // 2],
                                     ACT.Gelu, bias=b1_sb[:, 2 * k + i, f:f + 1]).then_inc(hid_ready, 1)
            act.wait_ge(got[NG - 1], 16 * TOPK)
            for k in range(TOPK):
                for j in range(TPG * (NG - 1), NT):
                    last = v.activation(picked[k][:, j, :], picked[k][:, j, :], ACT.Copy, scale=wk[:, k, j:j + 1])
                last.then_inc(weighted, 1)

        @block.vector
        def _(dve):
            v = nc.vector
            own = Chain(dve, chain_dve)
            v.memset(eps_col[:, :], EPS)
            v.memset(one_col[:, :], 1.0)
            dve.wait_ge(ids_in, 16)
            own.link(v.tensor_copy(idf[:, 0, :], ids_sb[:, :]))
            own.link(v.tensor_scalar(idf[:, 1, :], idf[:, 0, :], 0.0, float(VOCAB), ALU.is_lt, ALU.mult))
            own.link(v.tensor_tensor(idf[:, 0, :], idf[:, 0, :], idf[:, 1, :], ALU.add))
            own.link(v.tensor_scalar(idf[:, 0, :], idf[:, 0, :], 0.0, float(VOCAB - 1), ALU.max, ALU.min))
            v.tensor_copy(idx[:, :], idf[:, 0, :]).then_inc(idx_ready, 1)
            v.memset(bc[0:96, 0:ET * D], 0.0).then_inc(biases_zero, 1)
            v.memset(wbc[:, :, :, :], 0.0).then_inc(wbc_zero, 1)
            v.memset(bbc[:, :], 0.0).then_inc(wbc_zero, 1)
            v.memset(mean_w[:, :], 1.0 / D)
            v.memset(not_first[:, :, :], 1.0)
            own.mark(v.memset(cnt[:, :, :], 0.0))
            v.memset(ones_bf[:, :], 1.0)
            own.link(v.memset(sel[:, :, :], 0.0))
            v.memset(not_first[:, :, 0:1], 0.0).then_inc(filled, 1)
            bias, first, left, second = bc[0:96, 0:ET * D], split[1][:, 0:ET * D], rest[:, 0:ET * D], part[:, 0:ET * D]
            dve.wait_ge(biases_in, 16 * 3)
            own.link(v.tensor_copy(first, bias))
            own.link(v.tensor_tensor(left, bias, first, ALU.subtract))
            own.link(v.tensor_copy(second, left))
            own.link(v.tensor_tensor(left, left, second, ALU.subtract))
            v.tensor_copy(first[32:64, :], second[32:64, :])
            v.tensor_copy(first[64:96, :], left[64:96, :]).then_inc(biases_ready, 1)
            def gates(h):
                js = slice(h * NT // NSEQ, (h + 1) * NT // NSEQ)
                n = NT // NSEQ
                g, c, fl, ab, fr = [gate[:, i, js] for i in range(5)]
                raw = emb[:, js, D]
                dve.wait_ge(emb_in[h], 16 * n)
                own.link(v.tensor_scalar(g, raw, float(D), None, ALU.mult))
                def above(k):
                    return v.tensor_scalar(ge[:, js, k - 1], g, float(k * STEP - 1), None, ALU.is_gt)

                def between(k):
                    return v.tensor_tensor(oh[:, js, k], ge[:, js, k - 1], ge[:, js, k], ALU.subtract)

                n = own.mark(v.tensor_scalar(c, g, 1e9, None, ALU.mult))
                own.mark(above(1))
                own.need(n)
                n = own.mark(v.tensor_scalar(c, c, -EXACT, EXACT, ALU.max, ALU.min))
                own.mark(above(2))
                own.need(n)
                n = own.mark(v.tensor_copy(gate_i[:, js], c))
                own.mark(above(3))
                own.need(n)
                n = own.mark(v.tensor_copy(fl, gate_i[:, js]))
                own.mark(above(4))
                own.need(n)
                n = own.mark(v.tensor_tensor(ab, fl, c, ALU.is_gt))
                own.mark(v.tensor_scalar(oh[:, js, 0], ge[:, js, 0], -1.0, 1.0, ALU.mult, ALU.add))
                own.need(n)
                n = own.mark(v.tensor_tensor(fl, fl, ab, ALU.subtract))
                own.mark(between(1))
                own.need(n)
                n = own.mark(v.tensor_tensor(fr, c, fl, ALU.subtract))
                own.mark(between(2))
                own.need(n)
                own.mark(v.tensor_scalar(fr, fr, 1e-9, None, ALU.mult))
                own.mark(between(3))
                own.need(own.count)
                v.tensor_copy(oh[:, js, ET - 1], ge[:, js, ET - 2]).then_inc(gates_ready, 1)
                dve.wait_ge(gates_ready, h + 1)

            def moments(g):
                for j in range(TPG * g, TPG * (g + 1)):
                    n = own.mark(v.bn_stats(stats[:, j, :], tok[:, j, :]))
                own.need(n)
                for j in range(TPG * g, TPG * (g + 1)):
                    last = v.bn_aggr(mv[:, j, :], stats[:, j, :])
                return last

            def combine(g, pr_):
                dve.wait_ge(first_taken, 2 * g + pr_ + 1)
                b0 = 1 + 3 * pr_
                done = [0, 0]
                for e in range(1, ET):
                    for r in range(2):
                        j = TPG * g + 2 * pr_ + r
                        y = bank(b0 + r)[:, e * D:(e + 1) * D] if e < 4 else bank(b0 + 2)[:, r * D:(r + 1) * D]
                        if e > 1:
                            own.need(done[r])
                        ins = v.scalar_tensor_tensor(tok[:, j, :], y, oh[:, j, e:e + 1], tok[:, j, :],
                                                     ALU.mult, ALU.add)
                        if e == ET - 1 and r == 1:
                            ins.then_inc(combined, 1)
                        else:
                            done[r] = own.mark(ins)
                own.need(done[0])
                dve.wait_ge(combined, 2 * g + pr_ + 1)

            def shift(g):
                dve.wait_ge(rstd_ready, g + 1)
                js = slice(TPG * g, TPG * (g + 1))
                v.scalar_tensor_tensor(rstd[:, 2, js], mv[:, js, 0], -1.0, rstd[:, 0, js], ALU.mult, ALU.mult)\
                    .then_inc(shift_ready, 1)

            gates(0)
            mask(v, own, 0)
            mask(v, own, 1)
            dve.wait_ge(weights_in, 16 * N_LOADS)
            dve.wait_ge(ident_ready, 1)
            own.link(v.tensor_reduce(idf[:, 0, 0:NL], wmix[:, :, :], AX.X, ALU.add))
            own.link(v.tensor_scalar(idf[:, 0, 0:NL], idf[:, 0, 0:NL], 1.0 / D, None, ALU.mult))
            for l in range(NL):
                own.link(v.tensor_scalar(wmix[:, l, :], wmix[:, l, :], idf[:, 0, l:l + 1], None, ALU.subtract))
            dve.wait_ge(bmix_mean, 1)
            v.tensor_tensor(cols[:, 2, :], cols[:, 2, :], bank(7)[:, 0:NL], ALU.subtract).then_inc(mean_ready, 1)
            gates(1)
            for g in range(NG):
                combine(g, 0)
                if g > 0:
                    shift(g - 1)
                combine(g, 1)
                moments(g).then_inc(var_ready, 1)
            shift(NG - 1)

            def first_rest(p):
                dve.wait_ge(bc_ready, 2 * (p + 1))
                v.tensor_tensor(rest[:, 0:HALF], bc[0:96, 0:HALF], split[p % 2][:, 0:HALF], ALU.subtract)\
                    .then_inc(split_first, 1)

            def second_rest(p):
                dve.wait_ge(split_second, p + 1)
                v.tensor_tensor(split[p % 2][64:96, 0:HALF], rest[64:96, 0:HALF], part[64:96, 0:HALF], ALU.subtract)\
                    .then_inc(split_ready, 1)

            def normed(p, h=None):
                y, l = part_of(two_banks(p), h), p // NSEQ
                dve.wait_ge(rstd_psum, count(p, h))
                v.scalar_tensor_tensor(y, y, cols[:, 3, l:l + 1], part_of(work[:, 1, :], h), ALU.mult, ALU.mult)\
                    .then_inc(z_psum, 1)

            def residual(p, h=None):
                y, l = part_of(two_banks(p), h), p // NSEQ
                dve.wait_ge(z_psum, count(p, h))
                v.scalar_tensor_tensor(part_of(h_out(p), h), y, cols[:, 4, l:l + 1], part_of(h_in(p), h),
                                       ALU.add, ALU.add).then_inc(h_next, 1)

            def decoded(g):
                js = slice(TPG * g, TPG * (g + 1))
                dve.wait_ge(dec_psum, g + 1)
                dve.wait_ge(bdec_added, 1)
                v.tensor_tensor(tok[:, js, :], decoded_bank(g).rearrange("p (q d) -> p q d", d=D), tok[:, js, :],
                                ALU.add).then_inc(tok_done, 1)
                dve.wait_ge(tok_done, g + 1)
                moments(g).then_inc(var2_ready, 1)

            def normalise(g):
                dve.wait_ge(rstd2_ready, g + 1)
                dve.wait_ge(g_ready, H_RING + NS * (NPH - 1) + 3)
                for j in range(TPG * g, TPG * (g + 1)):
                    last = v.tensor_scalar(z2[:, j, 0:D], tok[:, j, :], mv[:, j, 0:1], rstd[:, 0, j:j + 1],
                                           ALU.subtract, ALU.mult)
                last.then_inc(z2_ready, 1)

            def router(r):
                tiles = ROUTED[r]
                js, n_tiles = slice(tiles.start, tiles.stop), len(tiles)
                bc_e = lambda x: x[:, None, :].broadcast_to([P, n_tiles, NE])
                bc_t = lambda x: x[:, :, None].broadcast_to([P, n_tiles, NE])
                by_tile = lambda x: x.rearrange("p (j e) -> p j e", e=NE)
                l_, p_ = lg[:, js, :], pr[:, js, :]
                top, total, inverse, pair_sum = [rmax[:, i, js] for i in range(4)]
                dve.wait_ge(logits_ready, r + 1)
                own.link(v.tensor_tensor(l_, by_tile(logits_bank[:, js.start * NE:js.stop * NE]), bc_e(br_bc),
                                         ALU.add))
                own.link(v.tensor_reduce(top, l_, AX.X, ALU.max))
                v.tensor_tensor(l_, l_, bc_t(top), ALU.subtract).then_inc(shifted, 1)
                dve.wait_ge(exped, r + 1)
                own.link(v.tensor_reduce(total, p_, AX.X, ALU.add))
                own.link(v.reciprocal(inverse, total))
                own.link(v.tensor_tensor(p_, p_, bc_t(inverse), ALU.mult))
                for j in tiles:
                    n = own.mark(v.max(m8[:, j, :], pr[:, j, :]))
                own.need(n)
                for j in tiles:
                    n = own.mark(v.max_index(i8[:, j, :], m8[:, j, :], pr[:, j, :]))
                own.need(n)
                own.link(v.tensor_copy(i8f[:, js, :], i8[:, js, 0:TOPK]))
                for k in range(TOPK):
                    n = own.mark(v.tensor_tensor(ohk[k][:, js, :], bc_e(iota_e), bc_t(i8f[:, js, k]), ALU.is_equal))
                own.need(n)
                v.tensor_tensor(routed[:, js, :], ohk[0][:, js, :], ohk[1][:, js, :], ALU.add).then_inc(counted, 1)
                dve.wait_ge(g_ready, H_RING + NS * (NPH - 1) + 3)
                own.link(v.tensor_copy(z2[:, js, D + 1], i8f[:, js, 0]))
                own.link(v.tensor_tensor(pair_sum, m8[:, js, 0], m8[:, js, 1], ALU.add))
                own.link(v.tensor_scalar(pair_sum, pair_sum, 1e-9, None, ALU.add))
                own.link(v.reciprocal(top, pair_sum))
                for k in range(TOPK):
                    n = own.mark(v.tensor_tensor(wk[:, k, js], m8[:, js, k], top, ALU.mult))
                dve.wait_ge(pos_ready, r + 1)
                own.link(v.tensor_copy(cnt[:, :, js], count_bank[:, NT * NE:(NT + n_tiles) * NE]
                                       .rearrange("p (j e) -> p e j", e=NE)))
                own.link(v.tensor_tensor_scan(cum[:, :, :].rearrange("p e j -> p (e j)"),
                                              not_first[:, :, :].rearrange("p e j -> p (e j)"),
                                              cnt[:, :, :].rearrange("p e j -> p (e j)"), 0.0, ALU.mult, ALU.add))
                own.link(v.tensor_tensor(cum[:, :, js], cum[:, :, js], cnt[:, :, js], ALU.subtract))
                own.link(v.tensor_tensor(pos[:, js, :], by_tile(count_bank[:, 0:n_tiles * NE]),
                                         cum[:, :, js].rearrange("p e j -> p j e"), ALU.add))
                own.link(v.tensor_tensor(slot[:, js, :], pos[:, js, :], bc_e(iota_cap), ALU.add))
                for i, (k, src, dst_) in enumerate((k, src, dst_) for k in range(TOPK)
                                                   for src, dst_ in ((pos, posk), (slot, slotk))):
                    own.mark(v.tensor_tensor(tmp4[i][:, 0:n_tiles, :], ohk[k][:, js, :], src[:, js, :], ALU.mult))
                own.need(own.count)
                for i, (k, dst_) in enumerate((k, dst_) for k in range(TOPK) for dst_ in (posk, slotk)):
                    own.mark(v.tensor_reduce(dst_[:, k, js], tmp4[i][:, 0:n_tiles, :], AX.X, ALU.add))
                own.need(own.count)
                own.link(v.tensor_scalar(keep[:, :, js], posk[:, :, js], float(CAP), None, ALU.is_lt))
                own.link(v.tensor_scalar(posk[:, :, js], keep[:, :, js], -float(2 * ROWS), float(2 * ROWS),
                                         ALU.mult, ALU.add))
                own.link(v.tensor_tensor(posk[:, :, js], posk[:, :, js], slotk[:, :, js], ALU.add))
                v.tensor_copy(into[:, :, js], posk[:, :, js]).then_inc(idx_made, 1)
                own.link(v.tensor_tensor(wk[:, :, js], wk[:, :, js], keep[:, :, js], ALU.mult))
                own.link(v.tensor_tensor(total, wk[:, 0, js], wk[:, 1, js], ALU.add))
                own.link(v.tensor_scalar(total, total, 1e-9, None, ALU.add))
                own.link(v.reciprocal(inverse, total))
                for k in range(TOPK):
                    own.link(v.tensor_tensor(wk[:, k, js], wk[:, k, js], inverse, ALU.mult))

            dve.sem_inc(scanned, A_RING)
            def step_size(p):
                dve.wait_ge(relu_done, p + 1)
                dve.wait_ge(dt_parts, p + 1)
                own.link(v.tensor_tensor(dt[:, p % 2, :], work[:, 0, :], work[:, 1, :], ALU.add))
                v.tensor_tensor(du[:, p % 2, :], dt[:, p % 2, :], h_in(p), ALU.mult).then_inc(dt_ready, 1)

            first_rest(0)
            second_rest(0)
            dve.wait_ge(z_ready, NG)
            v.tensor_tensor(tok[:, :, :], tok[:, :, :], bdec_bc[:, None, :].broadcast_to([P, NT, D]), ALU.add)\
                .then_inc(bdec_added, 1)
            step_size(0)
            dve.wait_ge(hT_ready, NG)
            for p in range(NPH):
                def pair(n, q, i, behind):
                    for r in range(2):
                        u = NS * p + n + r
                        dve.wait_ge(b_ready, u + 1)
                        dve.wait_ge(g_ready, u + 1)
                        v.tensor_tensor(h_ring[:, i + r, :], du[:, p % 2, :], bank(2 * r, 2), ALU.mult)\
                            .then_inc(u_done, 1)
                    for r in range(2):
                        u = NS * p + n + r
                        dve.wait_ge(u_done, u + 1)
                        dve.wait_ge(a_ready, u + 1)
                        v.tensor_tensor_scan(h_ring[:, i + r, :], a_ring[:, i + r, :], h_ring[:, i + r, :], 0.0,
                                             ALU.mult, ALU.add).then_inc(scanned, 1)
                        if r == 0:
                            behind(n)

                dve.wait_ge(dt_ready, p + 1)
                pieces = {}
                if p > 0:
                    for n, piece in zip(DVE_POST, (normed, residual)):
                        pieces.setdefault(n, []).append(lambda piece=piece: piece(p - 1))
                if p + 1 == NPH:
                    pieces.setdefault(DVE_ROUTER[0], []).append(lambda: [decoded(g) for g in range(NG // 2)])
                    pieces.setdefault(DVE_ROUTER[1], []).append(lambda: [normalise(g) for g in range(NG // 2)])
                if p + 1 < NPH:
                    for n, piece in zip(DVE_PREP, (first_rest, second_rest, step_size)):
                        pieces.setdefault(n, []).append(lambda piece=piece: piece(p + 1))
                units_of(dve, pieces, pair)
            router(0)
            for h in range(2):
                normed(NPH - 1, h)
                residual(NPH - 1, h)
            for g in range(NG // 2, NG):
                decoded(g)
            for g in range(NG // 2, NG):
                normalise(g)
            for r in range(1, len(ROUTED)):
                router(r)
            dve.sem_inc(out_copied, OUT_RING)
            dve.wait_ge(xeT_ready, 1)
            v.tensor_copy(xeT[0], bank(4, 2)[:, 0:CAP]).then_inc(xeT_copied, 1)

            def rows_next(e, i):
                dve.wait_ge(xeT_ready, e + 1)
                v.tensor_copy(xeT[i], bank(4, 2)[:, 0:CAP]).then_inc(xeT_copied, 1)

            def destinations(e, i):
                dve.wait_ge(rows_in[i], 8 * (e - i) + 16)
                dve.wait_ge(outputs_free, e + 1)
                v.tensor_scalar(is_second[:, :], xb[i][:, :, D + 1], iota_e[:, bass.ds(e, 1)], float(T),
                                ALU.not_equal, ALU.mult).then_inc(second_ready, 1)
                dve.wait_ge(second_ready, e + 1)
                v.scalar_tensor_tensor(dest[:, :], xb[i][:, :, D], float(FAR), is_second[:, :], ALU.add, ALU.add)\
                    .then_inc(dest_sum, 1)
                dve.wait_ge(dest_sum, e + 1)
                v.tensor_copy(dest_i[i][:, :], dest[:, :]).then_inc(dest_ready, 1)

            def output(e, i):
                destinations(e, i)
                for a, (t0, t1) in enumerate(PARTS):
                    dve.wait_ge(out_psum, 2 * e + a + 1)
                    v.tensor_tensor(ob[i][:, t0:t1, :], part_psum(a),
                                    b2_bc[:, bass.ds(e, 1), :].broadcast_to([P, t1 - t0, D]), ALU.add)\
                        .then_inc(out_copied, 1)

            with dve.Fori(0, NE // 2 - 1) as k:
                for i in range(2):
                    e = 2 * k
                    rows_next(e + i + 1, 1 - i)
                    output(e + i, i)
            rows_next(NE - 1, 1)
            for i in range(2):
                output(NE - 2 + i, i)
            for g in range(NG - 1):
                dve.wait_ge(got[g], 16 * TOPK)
                for k in range(TOPK):
                    for j in range(TPG * g, TPG * (g + 1)):
                        ins = v.scalar_tensor_tensor(out_sb[:, j, :], picked[k][:, j, :], wk[:, k, j:j + 1],
                                                     (tok if k == 0 else out_sb)[:, j, :], ALU.mult, ALU.add)
                        if k == 0:
                            own.mark(ins)
                        else:
                            ins.then_inc(out_ready, 1)
                    own.need(own.count)

        @block.tensor
        def _(pe):
            v = nc.tensor

            def mm(out_ap, lhsT, rhs, start=True, stop=True):
                return v.matmul(out_ap, lhsT, rhs, start=start, stop=stop)

            def wide(out_ap, lhsT, rhs, start=True, stop=True):
                for o, r in zip(halves(out_ap), halves(rhs)):
                    last = mm(o, lhsT, r, start, stop)
                return last

            pe.wait_ge(weights_in, 16 * N_LOADS)
            pe.wait_ge(filled, 1)
            mm(bank(7)[:, 0:NL], mean_w[:, :], cols[:, 2, :]).then_inc(bmix_mean, 1)

            def transpose_x(g):
                pe.wait_ge(masked[g // 2], g % 2 + 1)
                if g > 0:
                    pe.wait_ge(xT_copied, g)
                for q in range(TPG):
                    last = v.transpose(bank(0)[:, q * P:(q + 1) * P], xm[g % 2][:, q, :], ident[:, :])
                last.then_inc(xT_ready, 1)

            def all_experts(g, pr_):
                pe.wait_ge(xT_copied, g + 1)
                if g > 0:
                    pe.wait_ge(combined, 2 * (g - 1) + pr_ + 1)
                b0 = 1 + 3 * pr_
                for r in range(2):
                    x_ = xT[g % 2][:, (2 * pr_ + r) * P:(2 * pr_ + r + 1) * P]
                    for out_, es in ((bank(b0 + r), slice(0, 4)), (bank(b0 + 2)[:, r * D:(r + 1) * D], slice(4, 5))):
                        mm(out_, sel[0:96, 0, :], split[1][:, es.start * D:es.stop * D], True, False)
                        last = mm(out_, x_, tokw[:, es, :].rearrange("p e d -> p (e d)"), False, True)
                last.then_inc(y_tok_ready, 1)

            def transpose_z(g):
                pe.wait_ge(z_ready, g + 1)
                if g == 0:
                    pe.wait_ge(mean_ready, 1)
                else:
                    pe.wait_ge(hT_ready, g)
                for q in range(TPG):
                    last = v.transpose(bank(7)[:, q * P:(q + 1) * P], z[:, TPG * g + q, :], ident[:, :])
                last.then_inc(zT_ready, 1)

            pe.wait_ge(ident_ready, 1)
            pe.wait_ge(sel_ready, 1)
            pe.wait_ge(biases_ready, 1)
            pe.wait_ge(tok_in, 16)
            transpose_x(0)
            for g in range(NG):
                all_experts(g, 0)
                if g + 1 < NG:
                    transpose_x(g + 1)
                all_experts(g, 1)
                if g > 1:
                    transpose_z(g - 2)

            def project_dt(p, h):
                if p > 0 and h == 0:
                    pe.wait_ge(bc_ready, 2 * (p + 1))
                half = mm(halves(dt_banks(p))[h], wdt[:, p // NSEQ, :], halves(h_in(p))[h])
                if h == 1:
                    half.then_inc(dt_psum, 1)

            def project_bc(p, h):
                if p >= NSEQ and h == 0:
                    pe.wait_ge(h_next, p - NSEQ + 1)
                elif p > 0 and h == 0:
                    pe.wait_ge(hT_ready, NG)
                half = mm(bc_banks(p), wbc[:, p // NSEQ, h, :], halves(h_in(p))[h], h == 0, h == NSPLIT - 1)
                if h == NSPLIT - 1:
                    half.then_inc(bc_psum, 1)

            def mix_half(p, h):
                if h == 0:
                    pe.wait_ge(gelu_done, count(p, None))
                half = product(p, h, wmix[:, p // NSEQ, :])
                if h == 1:
                    half.then_inc(mixed, 1)

            def variance_half(p, h):
                if h == 0:
                    pe.wait_ge(squared, count(p, None))
                    pe.wait_ge(centred, count(p, None))
                half = product(p, h, mean_w[:, :])
                if h == 1:
                    half.then_inc(var_psum, 1)

            def spread_b(p, n, r):
                if NS * p + n >= 2:
                    pe.wait_ge(u_done, NS * p + n - 1)
                for h in range(2):
                    last = mm(bank(2 * r + h), sel[0:96, NS * h + n, :], split[p % 2][:, 0:HALF])
                last.then_inc(b_ready, 1)

            def add_y(p, n):
                if n == 0:
                    pe.wait_ge(dt_parts, p + 1)
                pe.wait_ge(g_ready, H_RING + NS * p + n + 1)
                if n == SKIP_UNIT:
                    pe.wait_ge(skip_added, p + 1)
                wide(two_banks(p), ident[:, :], g_ring[:, n % GU, :], n == 0, n == NS - 1).then_inc(y_added, 1)
                if n == NS - 1:
                    pe.wait_ge(y_added, G_RING + NS * (p + 1))
                    pe.sem_inc(y_ready, 1)

            def product(p, h, lhsT):
                return mm(halves(two_banks(p))[h], lhsT, halves(work[:, 0, :])[h])

            def mix(p, h):
                pe.wait_ge(gelu_done, count(p, h))
                product(p, h, wmix[:, p // NSEQ, :]).then_inc(mixed, 1)

            def variance(p, h):
                pe.wait_ge(squared, count(p, h))
                pe.wait_ge(centred, count(p, h))
                product(p, h, mean_w[:, :]).then_inc(var_psum, 1)

            def decode(h):
                for g in range(NG // 2 * h, NG // 2 * (h + 1)):
                    pe.wait_ge(h_next, NPH + g - NG // 2 if h else NPH - 1)
                    for q in range(TPG):
                        j = TPG * g + q
                        last = mm(decoded_bank(g)[:, q * D:(q + 1) * D], hT[NL % 2][:, j * P:(j + 1) * P], wdec[:, :])
                    last.then_inc(dec_psum, 1)

            def transpose_z2(h):
                for g in range(NG // 2 * h, NG // 2 * (h + 1)):
                    pe.wait_ge(z2_ready, g + 1)
                    for q in range(TPG):
                        last = v.transpose(z2T_bank(g)[:, q * P:(q + 1) * P], z2[:, TPG * g + q, 0:D], ident[:, :])
                    last.then_inc(z2T_ready, 1)

            def logits(r):
                if r:
                    pe.wait_ge(shifted, r)
                for j in ROUTED[r]:
                    g, q = divmod(j, TPG)
                    if q == 0:
                        pe.wait_ge(z2T_copied, g + 1)
                    last = mm(logits_bank[:, j * NE:(j + 1) * NE], work[:, g % 2, q * P:(q + 1) * P], wr[:, :])
                last.then_inc(logits_ready, 1)

            def positions(r):
                pe.wait_ge(counted, r + 1)
                if r:
                    pe.wait_ge(idx_made, r)
                n = len(ROUTED[r]) * NE
                r_ = routed[:, ROUTED[r].start:ROUTED[r].stop, :].rearrange("p j e -> p (j e)")
                mm(count_bank[:, 0:n], tri[:, :], r_)
                mm(count_bank[:, NT * NE:NT * NE + n], ones_bf[:, :], r_).then_inc(pos_ready, 1)

            pe.sem_inc(y_added, G_RING)
            pe.wait_ge(hT_ready, NG // NSEQ)
            pe.wait_ge(combined, 2 * NG - 1)
            pe.wait_ge(wbc_in, 16 * 8 * NSPLIT)
            for piece in (project_bc, project_dt):
                for h in range(2):
                    piece(0, h)
            for g in range(NG - 2, NG):
                transpose_z(g)
            pe.wait_ge(dt_parts, 1)
            pe.wait_ge(split_ready, 2)
            pe.wait_ge(consts_ready, 1)
            for r in range(2):
                spread_b(0, r, r)
            for p in range(NPH):
                pieces = {}
                if p > 0:
                    for i, (n, piece) in enumerate(zip(PE_POST, (mix_half, mix_half, variance_half, variance_half))):
                        pieces.setdefault(n, []).append(lambda piece=piece, h=i % 2: piece(p - 1, h))
                if p + 1 == NPH:
                    for n, piece in zip(PE_ROUTER, (decode, transpose_z2, logits)):
                        pieces.setdefault(n, []).append(lambda piece=piece: piece(0))
                if p + 1 < NPH:
                    for i, (n, piece) in enumerate(zip(PE_PREP, (project_bc, project_bc, project_dt, project_dt))):
                        pieces.setdefault(n, []).append(lambda piece=piece, h=i % 2: piece(p + 1, h))
                for n in range(NS):
                    ahead, behind = NS * p + n + 2, NS * p + n - Y_LAG
                    if ahead < NS * NPH:
                        if ahead % NS == 0:
                            pe.wait_ge(split_ready, 2 * (ahead // NS + 1))
                        spread_b(ahead // NS, ahead % NS, n % 2)
                    for piece in pieces.get(2 * n, []):
                        piece()
                    if behind >= 0:
                        add_y(behind // NS, behind % NS)
                    for piece in pieces.get(2 * n + 1, []):
                        piece()
            for n in range(NS - Y_LAG, NS):
                add_y(NPH - 1, n)
            positions(0)
            for piece in (mix, variance):
                for h in range(2):
                    piece(NPH - 1, h)
            decode(1)
            transpose_z2(1)
            for r in range(1, len(ROUTED)):
                logits(r)
                positions(r)

            def rows_in_(e, i):
                pe.wait_ge(rows_in[i], 8 * (e - i) + 16)
                for t in range(ST):
                    last = v.transpose(bank(4, 2)[:, t * P:(t + 1) * P], xb[i][:, t, 0:D], ident[:, :])
                last.then_inc(xeT_ready, 1)

            def hidden(e, i, f):
                if f == 0:
                    pe.wait_ge(xeT_copied, e + 1)
                    pe.wait_ge(w_in[i], 16 * (e - i) + 32)
                pe.wait_ge(hid_ready, FC * e + f + 1)
                for h in range(2):
                    last = mm(bank(2 * (f % 2) + h)[:, 0:CAP // 2], w1b[i][:, f * P:(f + 1) * P],
                              xeT[i][:, h * CAP // 2:(h + 1) * CAP // 2])
                last.then_inc(hid_psum, 1)

            def outputs(e, i):
                pe.wait_ge(hid_ready, FC * e + FC + HID_RING)
                for a, (t0, t1) in enumerate(PARTS):
                    pe.wait_ge(out_copied, 2 * e + a + 1)
                    for t in range(t0, t1):
                        for f in range(FC):
                            last = mm(part_psum(a)[:, t - t0, :], hid[i][:, f, t * P:(t + 1) * P], w2b[i][:, f, :],
                                      f == 0, f == FC - 1)
                    last.then_inc(out_psum, 1)

            def expert(e, i):
                for f in range(1, FC - 1):
                    hidden(e, i, f)
                rows_in_(e + 1, 1 - i)
                hidden(e, i, FC - 1)
                hidden(e + 1, 1 - i, 0)
                outputs(e, i)

            rows_in_(0, 0)
            hidden(0, 0, 0)
            with pe.Fori(0, NE // 2 - 1) as k:
                for i in range(2):
                    expert(2 * k + i, i)
            expert(NE - 2, 0)
            for f in range(1, FC):
                hidden(NE - 1, 1, f)
            outputs(NE - 1, 1)


def kernel(x, L0_tok_emb_table, L0_tok_gate_table, L0_tok_expert_w, L0_tok_expert_b, L0_attn_A_log, L0_attn_W_B,
           L0_attn_b_B, L0_attn_W_C, L0_attn_b_C, L0_attn_W_dt, L0_attn_b_dt, L0_attn_D_skip, L0_attn_W_mix,
           L0_attn_b_mix, L0_attn_ln_g, L0_attn_ln_b, L0_attn_W_dec, L0_attn_b_dec, L0_ffn_Wr, L0_ffn_br,
           L0_ffn_W1, L0_ffn_b1, L0_ffn_W2, L0_ffn_b2):
    import numpy as np
    import concourse.bacc as bacc
    from concourse import mybir as my
    from concourse.bass_utils import run_bass_kernel_spmd

    n = lambda a: np.asarray(a)
    B, S = n(x).shape
    E, D, F = n(L0_ffn_W1).shape
    feature_first = lambda a: n(a).swapaxes(0, 1)
    arrays = {
        "ids": n(x).reshape(-1, 128).T, "emb_gate": np.concatenate([n(L0_tok_emb_table), n(L0_tok_gate_table)], axis=1),
        "tok_w": n(L0_tok_expert_w).transpose(2, 0, 1),
        "tok_b": n(L0_tok_expert_b).reshape(1, -1),
        "A_log": feature_first(L0_attn_A_log), "W_B": feature_first(L0_attn_W_B), "b_B": n(L0_attn_b_B).T,
        "W_C": feature_first(L0_attn_W_C), "b_C": n(L0_attn_b_C).T, "W_dt": feature_first(L0_attn_W_dt),
        "b_dt": n(L0_attn_b_dt).T, "D_skip": n(L0_attn_D_skip).T, "W_mix": feature_first(L0_attn_W_mix),
        "b_mix": n(L0_attn_b_mix).T, "ln_g": n(L0_attn_ln_g).T, "ln_b": n(L0_attn_ln_b).T,
        "W_dec": n(L0_attn_W_dec), "b_dec": n(L0_attn_b_dec)[None, :], "Wr": n(L0_ffn_Wr),
        "br": n(L0_ffn_br)[None, :], "W1": n(L0_ffn_W1).transpose(1, 0, 2),
        "b1": n(L0_ffn_b1).reshape(E, F // 128, 128).transpose(2, 0, 1),
        "W2": n(L0_ffn_W2).reshape(E, F // 128, 128, D).transpose(2, 0, 1, 3).reshape(128, E, F // 128 * D),
        "b2": n(L0_ffn_b2)[None, :, :],
    }
    arrays = {k: np.ascontiguousarray(a) for k, a in arrays.items()}
    nc = bacc.Bacc("TRN2", target_bir_lowering=False, num_devices=1)
    args = [nc.dram_tensor("in_" + k, a.shape, my.dt.from_np(a.dtype), kind="ExternalInput").ap()
            for k, a in arrays.items()]
    out = nc.dram_tensor("out", [128, B * S // 128, D], my.dt.float32, kind="ExternalOutput").ap()
    tower_kernel(nc, *args, out)
    r = run_bass_kernel_spmd(nc, [{"in_" + k: a for k, a in arrays.items()}], core_ids=[0])
    got = r.results[0]["out"]
    return got.transpose(1, 0, 2).reshape(B, S, D)
```
